# Optimizing a Trainium2 kernel written in Bass

```python
import numpy as np
import jax
import jax.numpy as jnp

def _softmax(x, axis=-1):
    return jax.nn.softmax(x, axis=axis)

def _gelu(x):
    return jax.nn.gelu(x, approximate=True)

def _silu(x):
    return jax.nn.silu(x)

def _sigmoid(x):
    return jax.nn.sigmoid(x)

def _layernorm(x, axis=-1, eps=1e-05):
    m = jnp.mean(x, axis=axis, keepdims=True)
    v = jnp.var(x, axis=axis, keepdims=True)
    return (x - m) / jnp.sqrt(v + eps)

def _scatter_add(tgt, idx, src, axis=0):
    return tgt.at[idx].add(src)

def _segment_sum(src, seg, n):
    return jax.ops.segment_sum(src, seg, n)
kernel_name = 'mk_gnn_resnorm_d2_gnn_r32_7a5b5e'

def setup_inputs(seed: int=0):
    np.random.seed(seed)
    _w = jnp.asarray

    def _rec_inputs():
        import jax
        import jax.numpy as jnp
        _gk = jax.random.key(seed)
        x = -8.776e-05 + 1 * jax.random.normal(jax.random.fold_in(_gk, 1), (625, 256), jnp.float32)
        _s = jax.random.randint(jax.random.fold_in(_gk, 2), (10000,), 0, 625, jnp.int32)
        _d = jax.random.randint(jax.random.fold_in(_gk, 3), (10000,), 0, 625, jnp.int32)
        _loop = jnp.arange(625, dtype=jnp.int32)
        src = jnp.concatenate([_s, _d, _loop])
        dst = jnp.concatenate([_d, _s, _loop])
        _o = jnp.argsort(dst, stable=True)
        src = src[_o]
        dst = dst[_o]
        edge_attr_256 = -8.513e-05 + 0.999844 * jax.random.normal(jax.random.fold_in(_gk, 12), (20625, 256), jnp.float32)
        edge_attr_64 = 0.000312547 + 1.00004 * jax.random.normal(jax.random.fold_in(_gk, 13), (20625, 64), jnp.float32)
        return (x, src, dst, edge_attr_256, edge_attr_64)
    x, src, dst, edge_attr_256, edge_attr_64 = _rec_inputs()

    def _L0_gnn_setup():
        import jax, jax.numpy as jnp
        import numpy as np
        N_NODES = 625
        N_EDGES = 10000
        IN_F = 256
        OUT_F = 256
        EDGE_F = 256

        def _mlp2(x, W1, b1, W2, b2):
            return jax.nn.relu(x @ W1 + b1) @ W2 + b2
        key = jax.random.key(seed)
        ks = jax.random.split(key, 12)

        def lin(k, fan_in, shape):
            bound = 1.0 / np.sqrt(fan_in)
            return jax.random.uniform(k, shape, jnp.float32, -bound, bound)
        node_feat = jax.random.normal(ks[0], (N_NODES, IN_F), jnp.float32)
        edge_feat = jax.random.normal(ks[1], (N_EDGES, EDGE_F), jnp.float32)
        src = jax.random.randint(ks[2], (N_EDGES,), 0, N_NODES, jnp.int32)
        dst = jax.random.randint(ks[3], (N_EDGES,), 0, N_NODES, jnp.int32)
        We1 = lin(ks[4], EDGE_F, (EDGE_F, 2 * EDGE_F))
        be1 = lin(ks[5], EDGE_F, (2 * EDGE_F,))
        We2 = lin(ks[6], 2 * EDGE_F, (2 * EDGE_F, IN_F))
        be2 = lin(ks[7], 2 * EDGE_F, (IN_F,))
        Wn1 = lin(ks[8], IN_F, (IN_F, 2 * IN_F))
        bn1 = lin(ks[9], IN_F, (2 * IN_F,))
        Wn2 = lin(ks[10], 2 * IN_F, (2 * IN_F, OUT_F))
        bn2 = lin(ks[11], 2 * IN_F, (OUT_F,))
        eps = jnp.zeros((1,), jnp.float32)
        return {'node_feat': node_feat, 'edge_feat': edge_feat, 'src': src, 'dst': dst, 'We1': We1, 'be1': be1, 'We2': We2, 'be2': be2, 'Wn1': Wn1, 'bn1': bn1, 'Wn2': Wn2, 'bn2': bn2, 'eps': eps}
    _L0_gnn_all = _L0_gnn_setup()
    _L0_gnn_in = {k: v for k, v in _L0_gnn_all.items() if k in ('We1', 'be1', 'We2', 'be2', 'Wn1', 'bn1', 'Wn2', 'bn2', 'eps')}
    del _L0_gnn_all

    def _L1_gnn_setup():
        import jax, jax.numpy as jnp
        import numpy as np
        N, E, H, DE = (10000, 250000, 256, 64)
        EPS = 1e-05

        def _lin_init(k, fan_in, shape):
            s = 1.0 / np.sqrt(fan_in)
            return jax.random.uniform(k, shape, jnp.float32, -s, s)
        key = jax.random.key(seed)
        ks = jax.random.split(key, 12)
        x = jax.random.normal(ks[0], (N, H), jnp.float32)
        edge_index = jax.random.randint(ks[1], (2, E), 0, N)
        edge_attr = jax.random.normal(ks[2], (E, DE), jnp.float32)
        d_in = H + DE
        W1 = _lin_init(ks[3], d_in, (d_in, H))
        b1 = _lin_init(ks[4], d_in, (H,))
        W2 = _lin_init(ks[5], H, (H, H))
        b2 = _lin_init(ks[6], H, (H,))
        Wg = _lin_init(ks[7], d_in, (d_in, H))
        bg = _lin_init(ks[8], d_in, (H,))
        gamma = jnp.ones((H,), jnp.float32)
        beta = jnp.zeros((H,), jnp.float32)
        return {'x': x, 'edge_index': edge_index, 'edge_attr': edge_attr, 'W1': W1, 'b1': b1, 'W2': W2, 'b2': b2, 'Wg': Wg, 'bg': bg, 'gamma': gamma, 'beta': beta}
    _L1_gnn_all = _L1_gnn_setup()
    _L1_gnn_in = {k: v for k, v in _L1_gnn_all.items() if k in ('W1', 'b1', 'W2', 'b2', 'Wg', 'bg', 'gamma', 'beta')}
    del _L1_gnn_all
    return {'x': x, 'src': src, 'dst': dst, 'edge_attr_256': edge_attr_256, 'edge_attr_64': edge_attr_64, 'L0_gnn_We1': _L0_gnn_in['We1'], 'L0_gnn_be1': _L0_gnn_in['be1'], 'L0_gnn_We2': _L0_gnn_in['We2'], 'L0_gnn_be2': _L0_gnn_in['be2'], 'L0_gnn_Wn1': _L0_gnn_in['Wn1'], 'L0_gnn_bn1': _L0_gnn_in['bn1'], 'L0_gnn_Wn2': _L0_gnn_in['Wn2'], 'L0_gnn_bn2': _L0_gnn_in['bn2'], 'L0_gnn_eps': _L0_gnn_in['eps'], 'L1_gnn_W1': _L1_gnn_in['W1'], 'L1_gnn_b1': _L1_gnn_in['b1'], 'L1_gnn_W2': _L1_gnn_in['W2'], 'L1_gnn_b2': _L1_gnn_in['b2'], 'L1_gnn_Wg': _L1_gnn_in['Wg'], 'L1_gnn_bg': _L1_gnn_in['bg'], 'L1_gnn_gamma': _L1_gnn_in['gamma'], 'L1_gnn_beta': _L1_gnn_in['beta']}

def reference(x, src, dst, edge_attr_256, edge_attr_64, L0_gnn_We1, L0_gnn_be1, L0_gnn_We2, L0_gnn_be2, L0_gnn_Wn1, L0_gnn_bn1, L0_gnn_Wn2, L0_gnn_bn2, L0_gnn_eps, L1_gnn_W1, L1_gnn_b1, L1_gnn_W2, L1_gnn_b2, L1_gnn_Wg, L1_gnn_bg, L1_gnn_gamma, L1_gnn_beta):
    import jax
    import jax.numpy as jnp

    def _L0_gnn_ref(node_feat, edge_feat, src, dst, We1, be1, We2, be2, Wn1, bn1, Wn2, bn2, eps):
        import jax, jax.numpy as jnp
        import numpy as np
        N_NODES = 625
        N_EDGES = 10000
        IN_F = 256
        OUT_F = 256
        EDGE_F = 256

        def _mlp2(x, W1, b1, W2, b2):
            return jax.nn.relu(x @ W1 + b1) @ W2 + b2
        e = _mlp2(edge_feat, We1, be1, We2, be2)
        msg = jax.nn.relu(node_feat[src] + e)
        out_h = jax.ops.segment_sum(msg, dst, num_segments=N_NODES)
        out = _mlp2((1.0 + eps[0]) * node_feat + out_h, Wn1, bn1, Wn2, bn2)
        return out

    def _L1_gnn_ref(x, edge_index, edge_attr, W1, b1, W2, b2, Wg, bg, gamma, beta):
        import jax, jax.numpy as jnp
        import numpy as np
        N, E, H, DE = (10000, 250000, 256, 64)
        EPS = 1e-05

        def _lin_init(k, fan_in, shape):
            s = 1.0 / np.sqrt(fan_in)
            return jax.random.uniform(k, shape, jnp.float32, -s, s)
        src, dst = (edge_index[0], edge_index[1])
        ei = jnp.concatenate([x[src], edge_attr], axis=-1)
        core = jnp.maximum(ei @ W1 + b1, 0.0) @ W2 + b2
        gate = jax.nn.sigmoid(ei @ Wg + bg)
        msg = gate * core
        agg = jax.ops.segment_sum(msg, dst, num_segments=x.shape[0])
        out = agg + x
        mu = jnp.mean(out, axis=-1, keepdims=True)
        var = jnp.var(out, axis=-1, keepdims=True)
        out = (out - mu) * jax.lax.rsqrt(var + EPS) * gamma + beta
        return out
    edge_index = jnp.stack([src, dst])
    x = _layernorm(x + _L0_gnn_ref(x, edge_attr_256, src, dst, L0_gnn_We1, L0_gnn_be1, L0_gnn_We2, L0_gnn_be2, L0_gnn_Wn1, L0_gnn_bn1, L0_gnn_Wn2, L0_gnn_bn2, L0_gnn_eps), axis=-1)
    x = _layernorm(x + _L1_gnn_ref(x, edge_index, edge_attr_64, L1_gnn_W1, L1_gnn_b1, L1_gnn_W2, L1_gnn_b2, L1_gnn_Wg, L1_gnn_bg, L1_gnn_gamma, L1_gnn_beta), axis=-1)
    return x

_drawn_inputs = setup_inputs


def setup_inputs(seed=0):
    import zlib

    import numpy as np

    out = dict(_drawn_inputs(seed))
    spreads = {'L1_gnn_gamma': (1.0, 0.2), 'L1_gnn_beta': (0.0, 0.1)}
    factors = {'L0_gnn_be1': 5.742, 'L0_gnn_bn1': 8.0, 'L0_gnn_bn2': 8.0, 'L1_gnn_bg': 6.117}
    for name, (base, spread) in spreads.items():
        noise = np.random.default_rng([zlib.crc32(name.encode()), seed]).standard_normal(out[name].shape)
        drawn = base * np.exp(spread * noise) if base else spread * noise
        out[name] = jnp.asarray(drawn.astype(out[name].dtype))
    for name, factor in factors.items():
        out[name] = (out[name] * factor).astype(out[name].dtype)
    return out
```

```python
from contextlib import ExitStack

import concourse.bass as bass
from concourse import mybir

F32 = mybir.dt.float32
F32R = mybir.dt.float32r
I32 = mybir.dt.int32
U32 = mybir.dt.uint32
ALU = mybir.AluOpType
ACT = mybir.ActivationFunctionType
AX = mybir.AxisListType

P = 128
NODES = 625
NT = 5
NP = NODES // NT
NHALF = (320, 305)
EDGES = 20625
BLK = 512
TPB = BLK // P
NBLK = -(-EDGES // BLK)
TILES = NBLK * TPB
FULL_TILES = EDGES // P
TAIL = EDGES - FULL_TILES * P
D = 256
KD = D // P
HID = 512
KH = HID // P
DE = 64
WIN = 64
NWIN = -(-NODES // WIN)
ACC = NODES + WIN - 1
LN_EPS = 1e-5
PAD_DST = -100000
LAG = 5
PAIRS = (NBLK - LAG) // 2
assert LAG + 2 * PAIRS == NBLK and 2 * DE == P


def run_steps(eng, step, last, first=0, pairs=PAIRS):
    for b in range(first, LAG):
        step(b, b // 2, b % 2)
    with eng.Fori(0, pairs) as i:
        step(2 * i + LAG, i + LAG // 2, LAG % 2)
        step(2 * i + LAG + 1, i + (LAG + 1) // 2, (LAG + 1) % 2)
    for b in range(LAG + 2 * pairs, last + 1):
        step(b, b // 2, b % 2)


def at_least(b, k):
    return b >= k if isinstance(b, int) else True


def inside(b):
    return 0 <= b < NBLK if isinstance(b, int) else True


def gnn_two_layers(nc, x, xT, src, dst, dst_first, efT, eaT, We1, be1, We2, be2, Wn1, bn1, Wn2, bn2, eps,
                   W1, b1, W2, b2, Wg, bg, gamma, beta, out):
    with ExitStack() as ctx:
        def sb(name, shape, dt=F32):
            return ctx.enter_context(nc.sbuf_tensor(name, shape, dt))

        def sem(name):
            return ctx.enter_context(nc.semaphore(name))

        def two(name):
            return [sem(name + "0"), sem(name + "1")]

        xtab = nc.dram_tensor("xtab", [NODES, D], F32, kind="Internal").ap()
        ptab = nc.dram_tensor("ptab", [NODES, 2 * D], F32, kind="Internal").ap()

        we1_raw = sb("we1_raw", [P, KD, HID])
        we1 = [sb(f"we1_{n}", [P, KD, HID], F32R) for n in "hl"]
        we2 = [sb(f"we2_{n}", [P, KH, D], F32R) for n in "hl"]
        we2_raw = sb("we2_raw", [P, KH, D])
        w2_raw = sb("w2_raw", [P, KD, D])
        w2 = [sb(f"w2_{n}", [P, KD, D], F32R) for n in "hl"]
        wp_raw = sb("wp_raw", [P, 2 * D])
        wp_hi = sb("wp_hi", [P, 2 * D], F32R)
        wp = sb("wp", [P, 2 * D], F32R)
        wx = sb("wx", [P, KD, 2 * D])
        wn1 = sb("wn1", [P, KD, HID])
        wn2 = sb("wn2", [P, KH, D])
        b2pad_raw = sb("b2pad_raw", [P, D])
        b2hi = sb("b2hi", [P, D], F32R)
        b2lo = sb("b2lo", [P, D], F32R)
        ones_r = sb("ones_r", [P, P], F32R)
        be1c = sb("be1c", [P, KH])
        bn1c = sb("bn1c", [P, KH])
        be2b = sb("be2b", [P, D])
        bn2r = sb("bn2r", [1, D])
        bpr = sb("bpr", [1, 2 * D])
        ones1 = sb("ones1", [1, P])
        ones_f = sb("ones_f", [P, P])
        gamma_b = sb("gamma_b", [P, D])
        beta_b = sb("beta_b", [P, D])
        epsp1 = sb("epsp1", [P, 1])
        ident = sb("ident", [P, P])

        xn = sb("xn", [NP, NT, D])
        acc = sb("acc", [P, KD, ACC])
        hT = sb("hT", [P, KD, NODES])
        yn = sb("yn", [NP, NT, D])
        xb2 = yn
        x1 = sb("x1", [NP, NT, D])
        stats = sb("stats", [NP, NT, 6])
        mv = sb("mv", [NP, NT, 2])
        sd = sb("sd", [NP, NT])
        rstd = sb("rstd", [NP, NT])

        src_all = sb("src_all", [P, TILES], I32)
        src_slot = sb("src_slot", [P, 2, TPB], I32)
        dst_i = sb("dst_i", [P, TILES], I32)
        dst_f = sb("dst_f", [P, TILES])
        dst_r = sb("dst_r", [P, TILES])
        first_i = sb("first_i", [1, NBLK], I32)
        first_f = sb("first_f", [1, NBLK])
        clamp = sb("clamp", [P, TILES])
        off = sb("off", [P, 1])
        off_i = sb("off_i", [1, 1], I32)
        iota = sb("iota", [P, NWIN * WIN])

        raw = sb("raw", [P, 2, KD, BLK])
        xh = sb("xh", [P, 2, KD, BLK], F32R)
        xl = sb("xl", [P, 2, KD, BLK], F32R)
        hf = sb("hf", [P, 2, BLK])
        hh = sb("hh", [P, 2, KH, BLK], F32R)
        hl = sb("hl", [P, 2, KH, BLK], F32R)
        xg = sb("xg", [P, 2, TPB, 2 * D])
        mf_gate = sb("mf_gate", [P, 2, 2, TPB, D])
        mf = mf_gate[:, 0, :, :, :]
        gate = mf_gate[:, 1, :, :, :]
        mh = sb("mh", [P, 2, TPB, D], F32R)
        ml = sb("ml", [P, 2, TPB, D], F32R)
        r1T = xg[:, :, :, :].rearrange("p a t d -> p (a t d)")[:, 0:KH * NODES].rearrange("p (k n) -> p k n", k=KH)
        pt = mf_gate[0:NP, :, :, :, :].rearrange("p g a t d -> p (g a t d)")[:, 0:NT * 2 * D].rearrange("p (t d) -> p t d", t=NT)
        onehot = sb("onehot", [P, 2, TPB, WIN], F32R)

        bank = [ctx.enter_context(nc.psum_tensor(f"bank{i}", [P, 512], F32)) for i in range(8)]

        s_we1, s_we2, s_w2, s_wp = sem("s_we1"), sem("s_we2"), sem("s_w2"), sem("s_wp")
        s_b2, s_small, s_x, s_idx, s_src, s_nodew = sem("s_b2"), sem("s_small"), sem("s_x"), sem("s_idx"), sem("s_src"), sem("s_nodew")
        s_xtab, s_ptab, s_out = sem("s_xtab"), sem("s_ptab"), sem("s_out")
        pool_const, dve_const = sem("pool_const"), sem("dve_const")
        hi_w, lo_w = sem("hi_w"), sem("lo_w")
        xb2_ready, prep, base_ps, off_ps, flag_ready = sem("xb2_ready"), sem("prep"), sem("base_ps"), sem("off_ps"), sem("flag_ready")
        L = [{n: sem(f"{n}_l{k}") for n in
              ("hi_done", "lo_done", "h_mm", "h_evac", "hl_done", "z_mm", "m_done", "mh_done", "ml_done",
               "slot_done", "oh_done", "sc_mm", "acc_done", "u_mm", "hg_done", "t_mm", "rh_done", "rl_done",
               "gate_done", "sc_seen", "all_summed")} for k in range(2)]
        loaded = [two("loaded_l0_"), two("loaded_l1_")]
        gathered = [two("gathered_l0_"), two("gathered_l1_")]
        acc_zero, h0_ready, n1_mm, r1_done, n2_mm, y_done, ln, sq, x1_done = (sem(n) for n in (
            "acc_zero", "h0_ready", "n1_mm", "r1_done", "n2_mm", "y_done", "ln", "sq", "x1_done"))
        lnstep = sem("lnstep")
        xt_mm, xt_done, p_mm, p_done, fin_mm, fin_done, res_done = (sem(n) for n in (
            "xt_mm", "xt_done", "p_mm", "p_done", "fin_mm", "fin_done", "res_done"))

        block = ctx.enter_context(nc.Block())

        def rows(w, n):
            return w.rearrange("(k p) n -> p k n", p=P)

        @block.sync
        def _(sp):
            def load0(b, half, q):
                if at_least(b, 2):
                    sp.wait_ge(L[0]["lo_done"], b - 1)
                sp.dma_start(raw[:, q, :, :], efT[:, :, bass.ds(b * BLK, BLK)]).then_inc(loaded[0][q], 16)

            def load1(b, half, q):
                if at_least(b, 2):
                    sp.wait_ge(L[1]["lo_done"], b - 1)
                else:
                    sp.wait_ge(L[0]["lo_done"], NBLK)
                sp.dma_start(raw[0:DE, q, 0, :], eaT[:, bass.ds(b * BLK, BLK)]).then_inc(loaded[1][q], 16)
                sp.dma_start(raw[DE:P, q, 0, :], eaT[:, bass.ds(b * BLK, BLK)]).then_inc(loaded[1][q], 16)

            sp.dma_start(we1_raw[:, :, :], rows(We1, HID)).then_inc(s_we1, 16)
            load0(0, 0, 0)
            sp.dma_start(xn[:, :, :], x.rearrange("(t p) d -> p t d", p=NP)).then_inc(s_x, 16)
            sp.dma_start(be2b[:, :], be2.partition_broadcast(P)).then_inc(s_x, 16)
            sp.dma_start(dst_i[:, :], dst).then_inc(s_idx, 16)
            sp.dma_start(first_i[:, :], dst_first).then_inc(s_idx, 16)
            sp.dma_start(src_all[:, :], src).then_inc(s_src, 16)
            sp.dma_start(we2_raw[:, :, :], rows(We2, D)).then_inc(s_we2, 16)
            load0(1, 0, 1)
            sp.wait_ge(xb2_ready, NT)
            sp.dma_start(xtab.rearrange("(t p) d -> p t d", p=NP), xb2[:, :, :]).then_inc(s_xtab, 16)
            sp.dma_start(w2_raw[:, :, :], rows(W2, D)).then_inc(s_w2, 16)
            for h in range(2):
                for g, w in enumerate((W1, Wg)):
                    sp.dma_start(wp_raw[h * DE:(h + 1) * DE, g * D:(g + 1) * D], w[D:D + DE, :]).then_inc(s_wp, 16)
            sp.wait_ge(pool_const, 2)
            sp.dma_start(b2pad_raw[0:1, :], b2).then_inc(s_b2, 16)
            for g, w in enumerate((W1, Wg)):
                sp.dma_start(wx[:, :, g * D:(g + 1) * D], rows(w[0:D, :], D)).then_inc(s_nodew, 16)
            sp.dma_start(wn1[:, :, :], rows(Wn1, HID)).then_inc(s_nodew, 16)
            sp.dma_start(wn2[:, :, :], rows(Wn2, D)).then_inc(s_nodew, 16)
            sp.dma_start(hT[:, :, :], rows(xT, NODES)).then_inc(s_nodew, 16)
            sp.dma_start(bn2r[:, :], bn2).then_inc(s_nodew, 16)
            sp.dma_start(bpr[:, 0:D], b1).then_inc(s_nodew, 16)
            sp.dma_start(bpr[:, D:2 * D], bg).then_inc(s_nodew, 16)
            sp.dma_start(gamma_b[:, :], gamma.partition_broadcast(P)).then_inc(s_nodew, 16)
            sp.dma_start(beta_b[:, :], beta.partition_broadcast(P)).then_inc(s_nodew, 16)

            run_steps(sp, load0, NBLK - 1, first=2)

            load1(0, 0, 0)
            load1(1, 0, 1)
            sp.wait_ge(p_done, NT)
            sp.dma_start(ptab.rearrange("(t p) d -> p t d", p=NP), pt[:, :, :]).then_inc(s_ptab, 16)
            run_steps(sp, load1, NBLK - 1, first=2)

            sp.wait_ge(res_done, NT)
            sp.dma_start(out.rearrange("(t p) d -> p t d", p=NP), yn[:, :, :]).then_inc(s_out, 16)
            sp.wait_ge(s_out, 16)

        @block.gpsimd
        def _(pool):
            nc.gpsimd.iota(iota[:, :], [[1, NWIN * WIN]], base=0, channel_multiplier=0,
                           allow_small_or_imprecise_dtypes=True).then_inc(pool_const, 1)
            nc.gpsimd.memset(b2pad_raw[:, :], 0.0).then_inc(pool_const, 1)
            nc.gpsimd.memset(ident[:, :], 0.0).then_inc(pool_const, 1)
            pool.wait_ge(pool_const, 3)
            nc.gpsimd.affine_select(out=ident[:, :], in_=ident[:, :], compare_op=ALU.not_equal, fill=1.0, base=0,
                                    pattern=[[-1, P]], channel_multiplier=1).then_inc(pool_const, 1)

            def slots(k, b, q):
                nc.gpsimd.tensor_copy(src_slot[:, q, :], src_all[:, bass.ds(b * TPB, TPB)]).then_inc(L[k]["slot_done"], 1)

            def gather(k, b, half, q, table, width):
                if at_least(b, 1):
                    pool.wait_ge(gathered[k][1 - q], 64 * (half + (q == 1)))
                if at_least(b, 2):
                    pool.wait_ge(L[k]["m_done" if k == 0 else "t_mm"], (b - 1) * (2 if k == 0 else 1))
                    if k == 1:
                        pool.wait_ge(L[k]["gate_done"], b - 1)
                pool.wait_ge(L[k]["slot_done"], b + 1)
                if not isinstance(b, int) or b + 1 < NBLK:
                    slots(k, b + 1, 1 - q)
                else:
                    slots(k, 0, 1 - q)
                for t in range(TPB):
                    nc.gpsimd.indirect_dma_start(
                        xg[:, q, t, 0:width], None, table,
                        bass.IndirectOffsetOnAxis(ap=src_slot[:, q, t:t + 1].bitcast(U32), axis=0),
                    ).then_inc(gathered[k][q], 16)

            def lo(k, b, q, n):
                pool.wait_ge(L[k]["hi_done"], b + 1)
                if at_least(b, 2):
                    pool.wait_ge(L[k]["h_mm" if k == 0 else "u_mm"], (b - 1) * TPB)
                elif k == 1:
                    pool.wait_ge(L[0]["h_mm"], NBLK * KH)
                nc.gpsimd.tensor_tensor(xl[:, q, 0:n, :], raw[:, q, 0:n, :], xh[:, q, 0:n, :].bitcast(F32),
                                        ALU.subtract).then_inc(L[k]["lo_done"], 1)

            def step0(b, half, q):
                if inside(b):
                    gather(0, b, half, q, xtab, D)
                if inside(b + 1) if isinstance(b, int) else True:
                    lo(0, b + 1, 1 - q, KD)

            pool.wait_ge(s_src, 16)
            slots(0, 0, 0)
            pool.wait_ge(s_xtab, 16)
            lo(0, 0, 0, KD)
            run_steps(pool, step0, NBLK - 1, pairs=PAIRS - 1)

            def step1(b, half, q):
                gather(1, b, half, q, ptab, 2 * D)
                if not isinstance(b, int) or inside(b + 1):
                    lo(1, b + 1, 1 - q, 1)

            pool.wait_ge(gathered[0][0], 64 * ((NBLK + 1) // 2))
            pool.wait_ge(L[0]["slot_done"], NBLK + 1)
            slots(1, 0, 0)
            lo(1, 0, 0, 1)
            pool.wait_ge(L[0]["m_done"], 2 * NBLK)
            pool.wait_ge(s_ptab, 16)
            run_steps(pool, step1, NBLK - 1, pairs=PAIRS - 1)

        @block.scalar
        def _(act):
            act.dma_start(be1c[:, :], be1).then_inc(s_small, 16)
            act.dma_start(bn1c[:, :], bn1).then_inc(s_small, 16)
            act.dma_start(epsp1[:, :], eps.partition_broadcast(P)).then_inc(s_small, 16)

            def hi(k, b, half, q, n):
                act.wait_ge(loaded[k][q], (16 if k == 0 else 32) * (half + 1))
                if at_least(b, 2):
                    act.wait_ge(L[k]["h_mm" if k == 0 else "u_mm"], (b - 1) * TPB)
                    act.wait_ge(L[k]["lo_done"], b - 1)
                elif k == 1:
                    act.wait_ge(L[0]["h_mm"], NBLK * KH)
                nc.scalar.activation(xh[:, q, 0:n, :], raw[:, q, 0:n, :], ACT.Copy).then_inc(L[k]["hi_done"], 1)

            act.wait_ge(s_we1, 16)
            nc.scalar.activation(we1[0][:, :, :], we1_raw[:, :, :],
                                 ACT.Copy).then_inc(hi_w, 1)
            hi(0, 0, 0, 0, KD)
            act.wait_ge(s_we2, 16)
            nc.scalar.activation(we2[0][:, :, :], we2_raw[:, :, :], ACT.Copy).then_inc(hi_w, 1)
            act.wait_ge(s_small, 48)

            def h_chunk(b, q, m):
                n = TPB * b + m
                act.wait_ge(L[0]["h_mm"], n + 1)
                if at_least(b, 2):
                    act.wait_ge(L[0]["z_mm"], 2 * (b - 1))
                nc.scalar.activation(hh[:, q, m, :], bank[m][:, :], ACT.Relu, bias=be1c[:, m:m + 1])
                if m >= 2 or at_least(b, 1):
                    act.wait_ge(L[0]["hl_done"], n - 1)
                nc.scalar.activation(hf[:, m % 2, :], bank[m][:, :], ACT.Relu, bias=be1c[:, m:m + 1]).then_inc(L[0]["h_evac"], 1)

            def mh0(b, q):
                for c in range(2):
                    act.wait_ge(L[0]["m_done"], 2 * b + c + 1)
                    if at_least(b, 2):
                        act.wait_ge(L[0]["sc_seen"], b - 1)
                    nc.scalar.activation(mh[:, q, 2 * c:2 * c + 2, :], mf[:, q, 2 * c:2 * c + 2, :], ACT.Relu).then_inc(L[0]["mh_done"], 1)

            def step0(b, half, q):
                if inside(b):
                    h_chunk(b, q, 0)
                if not isinstance(b, int) or b + 1 < NBLK:
                    hi(0, b + 1, half + (q == 1), 1 - q, KD)
                if inside(b):
                    for m in range(1, KH):
                        h_chunk(b, q, m)
                if inside(b - 1):
                    mh0(b - 1, 1 - q)

            run_steps(act, step0, NBLK + 0, pairs=PAIRS - 1)

            act.wait_ge(s_w2, 16)
            nc.scalar.activation(w2[0][:, :, :], w2_raw[:, :, :], ACT.Copy).then_inc(hi_w, 1)
            act.wait_ge(s_wp, 64)
            nc.scalar.activation(wp_hi[:, :], wp_raw[:, :], ACT.Copy).then_inc(hi_w, 1)
            act.wait_ge(s_b2, 16)
            nc.scalar.activation(b2hi[:, :], b2pad_raw[:, :], ACT.Copy).then_inc(hi_w, 1)
            hi(1, 0, 0, 0, 1)

            for m in range(KH):
                act.wait_ge(n1_mm, m + 1)
                nc.scalar.activation(r1T[:, m, 0:NHALF[0]], bank[2 * (m % 2)][:, 0:NHALF[0]], ACT.Relu, bias=bn1c[:, m:m + 1]).then_inc(r1_done, 1)
                nc.scalar.activation(r1T[:, m, NHALF[0]:NODES], bank[2 * (m % 2) + 1][:, 0:NHALF[1]], ACT.Relu, bias=bn1c[:, m:m + 1]).then_inc(r1_done, 1)

            def roots(k):
                act.wait_ge(ln, k)
                nc.scalar.activation(sd[:, :], mv[:, :, 1], ACT.Sqrt).then_inc(sq, 1)

            roots(1)

            def gates(b, half, q):
                act.wait_ge(L[1]["hg_done"], TPB * (b + 1))
                if at_least(b, 2):
                    act.wait_ge(L[1]["m_done"], 2 * (b - 1))
                nc.scalar.activation(gate[:, q, :, :], xg[:, q, :, D:2 * D], ACT.Sigmoid).then_inc(L[1]["gate_done"], 1)

            def rh(b, q):
                for k in range(KD):
                    act.wait_ge(L[1]["t_mm"], b + 1)
                    if at_least(b, 2):
                        act.wait_ge(L[1]["z_mm"], 2 * (b - 1))
                    nc.scalar.activation(hh[:, q, k, :], bank[2 + k][:, :], ACT.Relu).then_inc(L[1]["rh_done"], 1)

            def mh1(b, q):
                for c in range(2):
                    act.wait_ge(L[1]["m_done"], 2 * b + c + 1)
                    if at_least(b, 2):
                        act.wait_ge(L[1]["sc_seen"], b - 1)
                    nc.scalar.activation(mh[:, q, 2 * c:2 * c + 2, :], mf[:, q, 2 * c:2 * c + 2, :], ACT.Copy).then_inc(L[1]["mh_done"], 1)

            def step1(b, half, q):
                if not isinstance(b, int) or b + 1 < NBLK:
                    hi(1, b + 1, half + (q == 1), 1 - q, 1)
                if inside(b - 1):
                    gates(b - 1, half, 1 - q)
                if inside(b - 2):
                    mh1(b - 2, q)
                if inside(b - 1):
                    rh(b - 1, 1 - q)

            run_steps(act, step1, NBLK + 1, pairs=PAIRS - 1)
            roots(2)
            roots(3)

        @block.tensor
        def _(pe):
            pe.wait_ge(prep, 2)
            nc.tensor.matmul(bank[6][:, 0:NBLK], ones1[0:1, :], first_f[0:1, :], start=True, stop=True).then_inc(base_ps, 1)
            pe.wait_ge(prep, 8)
            nc.tensor.matmul(bank[7][:, 0:1], ones_f[:, :], off[:, :], start=True, stop=True).then_inc(off_ps, 1)
            pe.wait_ge(flag_ready, 1)
            outside = pe.value_load(off_i[0:1, 0:1], min_val=0, max_val=1)

            def scatter(k, b, q, gen):
                S = L[k]
                pe.wait_ge(S["mh_done"], 2 * b + 2)
                pe.wait_ge(S["ml_done"], 2 * b + 2)
                for w in range(NWIN if gen else 1):
                    n = NWIN * b + w if gen else b
                    u = w % 2 if gen else q
                    pe.wait_ge(S["oh_done"], n + 1)
                    if at_least(b, 2) or w >= 2 or (gen and at_least(b, 1)):
                        pe.wait_ge(S["acc_done"], n - 1)
                    for f in range(KD):
                        for t in range(TPB):
                            for part, m in enumerate((mh, ml)):
                                mm = nc.tensor.matmul(bank[6 + u][:, f * WIN:(f + 1) * WIN], m[:, q, t, f * P:(f + 1) * P],
                                                      onehot[:, u, t, :], start=(t == 0 and part == 0),
                                                      stop=(t == TPB - 1 and part == 1))
                    mm.then_inc(S["sc_mm"], 1)

            def h_mm(b, q):
                pe.wait_ge(L[0]["hi_done"], b + 1)
                pe.wait_ge(L[0]["lo_done"], b + 1)
                for m in range(KH):
                    if at_least(b, 1):
                        pe.wait_ge(L[0]["h_evac"], TPB * (b - 1) + m + 1)
                    passes = [(k, w, v) for k in range(KD) for w, v in ((0, xh), (0, xl), (1, xh))]
                    for n, (k, w, v) in enumerate(passes):
                        mm = nc.tensor.matmul(bank[m][:, :], we1[w][:, k, m * P:(m + 1) * P], v[:, q, k, :],
                                              start=(n == 0), stop=(n == len(passes) - 1))
                    mm.then_inc(L[0]["h_mm"], 1)

            def z_mm(b, q):
                pe.wait_ge(L[0]["hl_done"], TPB * (b + 1))
                for c in range(2):
                    if at_least(b, 1):
                        pe.wait_ge(L[0]["m_done"], 2 * (b - 1) + c + 1)
                    for t in (2 * c, 2 * c + 1):
                        passes = [(k, w, v) for k in range(KH) for v, w in ((hh, 0), (hh, 1), (hl, 0))]
                        for n, (k, w, v) in enumerate(passes):
                            mm = nc.tensor.matmul(bank[4 + c][:, (t % 2) * D:(t % 2 + 1) * D], v[:, q, k, t * P:(t + 1) * P],
                                                  we2[w][:, k, :], start=(n == 0), stop=(n == len(passes) - 1))
                    mm.then_inc(L[0]["z_mm"], 1)

            def layer0(gen):
                def step(b, half, q):
                    if inside(b):
                        h_mm(b, q)
                    if inside(b - 1):
                        z_mm(b - 1, 1 - q)
                    if inside(b - 2):
                        scatter(0, b - 2, q, gen)
                run_steps(pe, step, NBLK + 1)

            pe.wait_ge(hi_w, 2)
            pe.wait_ge(lo_w, 2)
            pe.wait_ge(off_ps, 1)
            with pe.If(outside < 1):
                layer0(False)
            with pe.Else():
                layer0(True)

            pe.wait_ge(s_nodew, 16 * 10)
            pe.wait_ge(h0_ready, 1)
            starts = (0, NHALF[0])
            for m in range(KH):
                if m >= 2:
                    pe.wait_ge(r1_done, 2 * (m - 1))
                for c in range(2):
                    for k in range(KD):
                        mm = nc.tensor.matmul(bank[2 * (m % 2) + c][:, 0:NHALF[c]], wn1[:, k, m * P:(m + 1) * P],
                                              hT[:, k, starts[c]:starts[c] + NHALF[c]], start=(k == 0), stop=(k == KD - 1))
                mm.then_inc(n1_mm, 1)
            pe.wait_ge(r1_done, 2 * KH)
            for t in range(NT):
                if t >= 2:
                    pe.wait_ge(y_done, t - 1)
                nc.tensor.matmul(bank[4 + t % 2][0:NP, 0:D], ones1[0:1, 0:NP], bn2r[:, :], start=True, stop=False)
                for k in range(KH):
                    mm = nc.tensor.matmul(bank[4 + t % 2][0:NP, 0:D], r1T[:, k, t * NP:(t + 1) * NP], wn2[:, k, :],
                                          start=False, stop=(k == KH - 1))
                mm.then_inc(n2_mm, 1)
            for t in range(NT):
                pe.wait_ge(x1_done, t + 1)
                if t >= 2:
                    pe.wait_ge(xt_done, t - 1)
                for k in range(KD):
                    mm = nc.tensor.transpose(bank[t % 2][:, k * P:k * P + NP], x1[:, t, k * P:(k + 1) * P], ident[0:NP, 0:NP])
                mm.then_inc(xt_mm, 1)
            for t in range(NT):
                pe.wait_ge(xt_done, t + 1)
                if t >= 2:
                    pe.wait_ge(p_done, t - 1)
                nc.tensor.matmul(bank[2 + t % 2][0:NP, :], ones1[0:1, 0:NP], bpr[:, :], start=True, stop=False)
                for k in range(KD):
                    mm = nc.tensor.matmul(bank[2 + t % 2][0:NP, :], hT[:, k, t * NP:(t + 1) * NP], wx[:, k, :],
                                          start=False, stop=(k == KD - 1))
                mm.then_inc(p_mm, 1)

            def u_tile(b, q, t):
                if t == 0:
                    pe.wait_ge(L[1]["hi_done"], b + 1)
                    pe.wait_ge(L[1]["lo_done"], b + 1)
                if t >= 2 or at_least(b, 1):
                    pe.wait_ge(L[1]["hg_done"], TPB * b + t - 1)
                for n, v in enumerate((xh, xl)):
                    mm = nc.tensor.matmul(bank[t % 2][:, :], v[:, q, 0, t * P:(t + 1) * P], wp[:, :], start=(n == 0), stop=(n == 1))
                mm.then_inc(L[1]["u_mm"], 1)

            def c_tile(b, q, t):
                c = t // 2
                if t == 0:
                    pe.wait_ge(L[1]["rl_done"], KD * (b + 1))
                if t % 2 == 0 and at_least(b, 1):
                    pe.wait_ge(L[1]["m_done"], 2 * (b - 1) + c + 1)
                passes = [(ones_r[:, :], b2hi[:, :]), (ones_r[:, :], b2lo[:, :])]
                passes += [(v[:, q, k, t * P:(t + 1) * P], w2[w][:, k, :]) for k in range(KD) for v, w in ((hh, 0), (hh, 1), (hl, 0))]
                for n, (lhs, rhs) in enumerate(passes):
                    mm = nc.tensor.matmul(bank[4 + c][:, (t % 2) * D:(t % 2 + 1) * D], lhs, rhs, start=(n == 0), stop=(n == len(passes) - 1))
                if t % 2:
                    mm.then_inc(L[1]["z_mm"], 1)

            def t_mm(b, q):
                pe.wait_ge(L[1]["hg_done"], TPB * (b + 1))
                if at_least(b, 1):
                    pe.wait_ge(L[1]["rl_done"], KD * b)
                for k in range(KD):
                    for t in range(TPB):
                        mm = nc.tensor.transpose(bank[2 + k][:, t * P:(t + 1) * P], xg[:, q, t, k * P:(k + 1) * P], ident[:, :])
                mm.then_inc(L[1]["t_mm"], 1)

            def layer1(gen):
                def step(b, half, q):
                    for t in range(TPB):
                        if inside(b):
                            u_tile(b, q, t)
                        if inside(b - 2):
                            c_tile(b - 2, q, t)
                    if inside(b - 1):
                        t_mm(b - 1, 1 - q)
                    if inside(b - 3):
                        scatter(1, b - 3, 1 - q, gen)
                run_steps(pe, step, NBLK + 2)

            pe.wait_ge(hi_w, 5)
            pe.wait_ge(lo_w, 5)
            with pe.If(outside < 1):
                layer1(False)
            with pe.Else():
                layer1(True)

            pe.wait_ge(L[1]["all_summed"], 1)
            for t in range(NT):
                if t >= 2:
                    pe.wait_ge(fin_done, t - 1)
                for k in range(KD):
                    mm = nc.tensor.transpose(bank[t % 2][0:NP, k * P:(k + 1) * P], acc[:, k, t * NP:(t + 1) * NP], ident[:, :])
                mm.then_inc(fin_mm, 1)

        @block.vector
        def _(dve):
            nprep = [0]

            def p_step(ins):
                nprep[0] += 1
                ins.then_inc(prep, 1)
                dve.wait_ge(prep, nprep[0])

            p_step(nc.vector.memset(ones1[:, :], 1.0))
            dve.wait_ge(s_idx, 32)
            p_step(nc.vector.tensor_copy(first_f[:, :], first_i[:, :]))
            nc.vector.memset(ones_f[:, :], 1.0)
            dve.wait_ge(s_x, 32)
            for t in range(NT):
                nc.vector.tensor_tensor(xb2[:, t, :], xn[:, t, :], be2b[0:NP, :], ALU.add).then_inc(xb2_ready, 1)
            p_step(nc.vector.tensor_copy(dst_f[:, :], dst_i[:, :]))
            dve.wait_ge(base_ps, 1)
            p_step(nc.vector.tensor_tensor(dst_r[:, :].rearrange("p (b t) -> p b t", t=TPB),
                                           dst_f[:, :].rearrange("p (b t) -> p b t", t=TPB),
                                           bank[6][:, 0:NBLK].rearrange("p (b o) -> p b o", o=1).broadcast_to([P, NBLK, TPB]), ALU.subtract))
            p_step(nc.vector.tensor_scalar(clamp[:, :], dst_r[:, :], 0.0, float(WIN - 1), ALU.max, ALU.min))
            p_step(nc.vector.tensor_tensor(clamp[:, :], clamp[:, :], dst_r[:, :], ALU.not_equal))
            p_step(nc.vector.tensor_reduce(off[:, :], clamp[:, 0:FULL_TILES], AX.X, ALU.add))
            p_step(nc.vector.tensor_tensor(off[0:TAIL, :], off[0:TAIL, :], clamp[0:TAIL, FULL_TILES:FULL_TILES + 1], ALU.add))
            dve.wait_ge(off_ps, 1)
            nc.vector.tensor_scalar(off_i[:, :], bank[7][0:1, 0:1], 1.0, None, ALU.min).then_inc(flag_ready, 1)
            dve.wait_ge(hi_w, 1)
            nc.vector.tensor_tensor(we1[1][:, :, :], we1_raw[:, :, :],
                                    we1[0][:, :, :].bitcast(F32), ALU.subtract).then_inc(lo_w, 1)
            dve.wait_ge(hi_w, 2)
            nc.vector.tensor_tensor(we2[1][:, :, :], we2_raw[:, :, :], we2[0][:, :, :].bitcast(F32), ALU.subtract).then_inc(lo_w, 1)
            nc.vector.memset(acc[:, :, :], 0.0).then_inc(acc_zero, 1)
            dve.wait_ge(flag_ready, 1)
            outside = dve.value_load(off_i[0:1, 0:1], min_val=0, max_val=1)

            def one_hot(k, b, q, gen, w=0):
                S = L[k]
                n = NWIN * b + w if gen else b
                u = w % 2 if gen else q
                if at_least(b, 2) or w >= 2 or (gen and at_least(b, 1)):
                    dve.wait_ge(S["sc_mm"], n - 1)
                which = dst_f if gen else dst_r
                nc.vector.tensor_tensor(
                    onehot[:, u, :, :],
                    iota[:, w * WIN:(w + 1) * WIN].rearrange("p (o w) -> p o w", o=1).broadcast_to([P, TPB, WIN]),
                    which[:, bass.ds(b * TPB, TPB)].rearrange("p (t o) -> p t o", o=1).broadcast_to([P, TPB, WIN]),
                    ALU.is_equal).then_inc(S["oh_done"], 1)

            def add_window(k, b, q, gen, w=0):
                S = L[k]
                n = NWIN * b + w if gen else b
                u = w % 2 if gen else q
                dve.wait_ge(S["sc_mm"], n + 1)
                if w >= 1 or at_least(b, 1):
                    dve.wait_ge(S["acc_done"], n)
                else:
                    dve.wait_ge(acc_zero, k + 1)
                first = w * WIN if gen else dve.value_load(first_i[0:1, bass.ds(b, 1)], min_val=0, max_val=NODES - 1)
                width = min(WIN, ACC - w * WIN) if gen else WIN
                where = acc[:, :, first:first + width] if gen else acc[:, :, bass.ds(first, WIN)]
                nc.vector.tensor_tensor(
                    where, where, bank[6 + u][:, 0:KD * WIN].rearrange("p (f w) -> p f w", f=KD)[:, :, 0:width],
                    ALU.add).then_inc(S["acc_done"], 1)

            def scatter(k, b, q, gen):
                if gen:
                    for w in range(NWIN):
                        one_hot(k, b, q, gen, w)
                        add_window(k, b, q, gen, w)
                else:
                    add_window(k, b, q, gen)
                dve.wait_ge(L[k]["acc_done"], (NWIN * (b + 1)) if gen else b + 1)
                nc.vector.memset(off[:, :], 0.0).then_inc(L[k]["sc_seen"], 1)

            def hl_chunk(b, q, m):
                n = TPB * b + m
                dve.wait_ge(L[0]["h_evac"], n + 1)
                if at_least(b, 2):
                    dve.wait_ge(L[0]["z_mm"], 2 * (b - 1))
                nc.vector.tensor_tensor(hl[:, q, m, :], hf[:, m % 2, :], hh[:, q, m, :].bitcast(F32), ALU.subtract).then_inc(L[0]["hl_done"], 1)

            def m0(b, half, q, c):
                dve.wait_ge(L[0]["z_mm"], 2 * b + c + 1)
                if c == 0:
                    dve.wait_ge(gathered[0][q], 64 * (half + 1))
                nc.vector.tensor_tensor(mf[:, q, 2 * c:2 * c + 2, :], bank[4 + c][:, :].rearrange("p (t d) -> p t d", t=2),
                                        xg[:, q, 2 * c:2 * c + 2, 0:D], ALU.add).then_inc(L[0]["m_done"], 1)

            def ml0(b, q, c):
                dve.wait_ge(L[0]["mh_done"], 2 * b + c + 1)
                nc.vector.scalar_tensor_tensor(out=ml[:, q, 2 * c:2 * c + 2, :], in0=mf[:, q, 2 * c:2 * c + 2, :], scalar=0.0,
                                               in1=mh[:, q, 2 * c:2 * c + 2, :].bitcast(F32), op0=ALU.max,
                                               op1=ALU.subtract).then_inc(L[0]["ml_done"], 1)

            def layer0(gen):
                def step(b, half, q):
                    if inside(b - 1) and not gen:
                        one_hot(0, b - 1, 1 - q, gen)
                    if inside(b):
                        for m in range(KH):
                            hl_chunk(b, q, m)
                    if inside(b - 1):
                        hb = half - (q == 0)
                        m0(b - 1, hb, 1 - q, 0)
                        m0(b - 1, hb, 1 - q, 1)
                        ml0(b - 1, 1 - q, 0)
                        ml0(b - 1, 1 - q, 1)
                    if inside(b - 2):
                        scatter(0, b - 2, q, gen)
                run_steps(dve, step, NBLK + 1)

            with dve.If(outside < 1):
                layer0(False)
            with dve.Else():
                layer0(True)

            dve.wait_ge(s_small, 48)
            nc.vector.tensor_scalar(epsp1[:, :], epsp1[:, :], 1.0, None, ALU.add).then_inc(dve_const, 1)
            dve.wait_ge(dve_const, 1)
            dve.wait_ge(s_nodew, 16 * 10)
            nc.vector.scalar_tensor_tensor(out=hT[:, :, :], in0=hT[:, :, :], scalar=epsp1[:, 0:1], in1=acc[:, :, 0:NODES],
                                           op0=ALU.mult, op1=ALU.add).then_inc(h0_ready, 1)
            dve.wait_ge(h0_ready, 1)
            nc.vector.memset(acc[:, :, :], 0.0).then_inc(acc_zero, 1)
            dve.wait_ge(hi_w, 5)
            nc.vector.tensor_tensor(w2[1][:, :, :], w2_raw[:, :, :], w2[0][:, :, :].bitcast(F32), ALU.subtract).then_inc(lo_w, 1)
            nc.vector.tensor_copy(wp[0:DE, :], wp_hi[0:DE, :].bitcast(F32))
            nc.vector.tensor_tensor(wp[DE:P, :], wp_raw[DE:P, :], wp_hi[DE:P, :].bitcast(F32), ALU.subtract).then_inc(lo_w, 1)
            nc.vector.tensor_copy(ones_r[:, :], ones_f[:, :])
            nc.vector.tensor_tensor(b2lo[:, :], b2pad_raw[:, :], b2hi[:, :].bitcast(F32), ALU.subtract).then_inc(lo_w, 1)

            nln = [0]

            def link(ins):
                nln[0] += 1
                ins.then_inc(lnstep, 1)
                dve.wait_ge(lnstep, nln[0])

            def moments(k):
                for t in range(NT):
                    ins = nc.vector.bn_stats(stats[:, t, :], yn[:, t, :])
                link(ins)
                for t in range(NT):
                    ins = nc.vector.bn_aggr(mv[:, t, :], stats[:, t, :])
                link(ins)
                nc.vector.tensor_scalar(mv[:, :, 1], mv[:, :, 1], LN_EPS, None, ALU.add).then_inc(ln, 1)
                dve.wait_ge(sq, k)
                link(nc.vector.reciprocal(rstd[:, :], sd[:, :]))

            for t in range(NT):
                dve.wait_ge(n2_mm, t + 1)
                nc.vector.tensor_tensor(yn[:, t, :], bank[4 + t % 2][0:NP, 0:D], xn[:, t, :], ALU.add).then_inc(y_done, 1)
            dve.wait_ge(y_done, NT)
            moments(1)
            for t in range(NT):
                nc.vector.tensor_scalar(x1[:, t, :], yn[:, t, :], mv[:, t, 0:1], rstd[:, t:t + 1], ALU.subtract, ALU.mult).then_inc(x1_done, 1)
            for t in range(NT):
                dve.wait_ge(xt_mm, t + 1)
                nc.vector.tensor_copy(hT[:, :, t * NP:(t + 1) * NP],
                                      bank[t % 2][:, 0:KD * P].rearrange("p (k n) -> p k n", k=KD)[:, :, 0:NP]).then_inc(xt_done, 1)
            for t in range(NT):
                dve.wait_ge(p_mm, t + 1)
                nc.vector.tensor_copy(pt[:, t, :], bank[2 + t % 2][0:NP, :]).then_inc(p_done, 1)

            def hg(b, half, q, t):
                dve.wait_ge(L[1]["u_mm"], TPB * b + t + 1)
                if t == 0:
                    dve.wait_ge(gathered[1][q], 64 * (half + 1))
                nc.vector.tensor_tensor(xg[:, q, t, :], bank[t % 2][:, :], xg[:, q, t, :], ALU.add).then_inc(L[1]["hg_done"], 1)

            def rl(b, q):
                for k in range(KD):
                    dve.wait_ge(L[1]["rh_done"], KD * b + k + 1)
                    if at_least(b, 2):
                        dve.wait_ge(L[1]["z_mm"], 2 * (b - 1))
                    nc.vector.scalar_tensor_tensor(out=hl[:, q, k, :], in0=bank[2 + k][:, :], scalar=0.0, in1=hh[:, q, k, :].bitcast(F32),
                                                   op0=ALU.max, op1=ALU.subtract).then_inc(L[1]["rl_done"], 1)

            def m1(b, q, c):
                dve.wait_ge(L[1]["z_mm"], 2 * b + c + 1)
                dve.wait_ge(L[1]["gate_done"], b + 1)
                nc.vector.tensor_tensor(mf[:, q, 2 * c:2 * c + 2, :], bank[4 + c][:, :].rearrange("p (t d) -> p t d", t=2),
                                        gate[:, q, 2 * c:2 * c + 2, :], ALU.mult).then_inc(L[1]["m_done"], 1)

            def ml1(b, q, c):
                dve.wait_ge(L[1]["mh_done"], 2 * b + c + 1)
                nc.vector.tensor_tensor(ml[:, q, 2 * c:2 * c + 2, :], mf[:, q, 2 * c:2 * c + 2, :],
                                        mh[:, q, 2 * c:2 * c + 2, :].bitcast(F32), ALU.subtract).then_inc(L[1]["ml_done"], 1)

            def layer1(gen):
                def step(b, half, q):
                    if inside(b):
                        hg(b, half, q, 0)
                        hg(b, half, q, 1)
                    if inside(b - 2):
                        m1(b - 2, q, 0)
                    if inside(b):
                        hg(b, half, q, 2)
                        hg(b, half, q, 3)
                    if inside(b - 2):
                        m1(b - 2, q, 1)
                        if not gen:
                            one_hot(1, b - 2, q, gen)
                        ml1(b - 2, q, 0)
                        ml1(b - 2, q, 1)
                    if inside(b - 1):
                        rl(b - 1, 1 - q)
                    if inside(b - 3):
                        scatter(1, b - 3, 1 - q, gen)
                run_steps(dve, step, NBLK + 2)

            with dve.If(outside < 1):
                layer1(False)
            with dve.Else():
                layer1(True)
            nc.vector.memset(clamp[:, :], 0.0).then_inc(L[1]["all_summed"], 1)

            for t in range(NT):
                dve.wait_ge(fin_mm, t + 1)
                nc.vector.tensor_tensor(yn[:, t, :], bank[t % 2][0:NP, 0:D], x1[:, t, :], ALU.add).then_inc(fin_done, 1)
            dve.wait_ge(fin_done, NT)
            moments(2)
            for t in range(NT):
                link(nc.vector.tensor_scalar(yn[:, t, :], yn[:, t, :], mv[:, t, 0:1], rstd[:, t:t + 1], ALU.subtract, ALU.mult))
                link(nc.vector.tensor_tensor(yn[:, t, :], yn[:, t, :], gamma_b[0:NP, :], ALU.mult))
                link(nc.vector.tensor_tensor(yn[:, t, :], yn[:, t, :], beta_b[0:NP, :], ALU.add))
                link(nc.vector.tensor_tensor(yn[:, t, :], yn[:, t, :], x1[:, t, :], ALU.add))
            moments(3)
            for t in range(NT):
                nc.vector.tensor_scalar(yn[:, t, :], yn[:, t, :], mv[:, t, 0:1], rstd[:, t:t + 1], ALU.subtract, ALU.mult).then_inc(res_done, 1)


def kernel(**inputs):
    import numpy as np
    import concourse.bacc as bacc
    from concourse.bass_utils import run_bass_kernel_spmd

    a = {k: np.ascontiguousarray(v) for k, v in inputs.items()}
    pad = NBLK * BLK - EDGES

    def edge_tiles(v, fill):
        return np.ascontiguousarray(np.concatenate([v, np.full(pad, fill, v.dtype)]).reshape(TILES, P).T)

    def edges_last(v):
        return np.ascontiguousarray(np.concatenate([v, np.zeros((pad, v.shape[1]), v.dtype)]).T)

    l0, l1 = "L0_gnn_", "L1_gnn_"
    arrays = {
        "x": a["x"], "xT": np.ascontiguousarray(a["x"].T),
        "src": edge_tiles(a["src"], 0), "dst": edge_tiles(a["dst"], PAD_DST),
        "dst_first": np.ascontiguousarray(a["dst"][::BLK])[None, :],
        "efT": np.ascontiguousarray(edges_last(a["edge_attr_256"]).reshape(KD, P, NBLK * BLK).transpose(1, 0, 2)),
        "eaT": edges_last(a["edge_attr_64"]),
        "We1": a[l0 + "We1"], "be1": np.ascontiguousarray(a[l0 + "be1"].reshape(KH, P).T),
        "We2": a[l0 + "We2"], "be2": a[l0 + "be2"],
        "Wn1": a[l0 + "Wn1"], "bn1": np.ascontiguousarray(a[l0 + "bn1"].reshape(KH, P).T),
        "Wn2": a[l0 + "Wn2"], "bn2": a[l0 + "bn2"][None, :], "eps": a[l0 + "eps"],
        "W1": a[l1 + "W1"], "b1": a[l1 + "b1"][None, :], "W2": a[l1 + "W2"], "b2": a[l1 + "b2"][None, :],
        "Wg": a[l1 + "Wg"], "bg": a[l1 + "bg"][None, :], "gamma": a[l1 + "gamma"], "beta": a[l1 + "beta"],
    }
    nc = bacc.Bacc("TRN2", target_bir_lowering=False, num_devices=1)
    arrays = {f"in_{k}": v for k, v in arrays.items()}
    aps = [nc.dram_tensor(k, v.shape, mybir.dt.from_np(v.dtype), kind="ExternalInput").ap() for k, v in arrays.items()]
    aps.append(nc.dram_tensor("out_0", (NODES, D), F32, kind="ExternalOutput").ap())
    gnn_two_layers(nc, *aps)
    r = run_bass_kernel_spmd(nc, [arrays], core_ids=[0])
    return r.results[0]["out_0"]
```

```python
from contextlib import ExitStack

import concourse.bass as bass
from concourse import mybir

F32 = mybir.dt.float32
F32R = mybir.dt.float32r
BF16 = mybir.dt.bfloat16
I32 = mybir.dt.int32
U32 = mybir.dt.uint32
ALU = mybir.AluOpType
ACT = mybir.ActivationFunctionType
AX = mybir.AxisListType

P = 128
NODES = 625
NT = 5
NP = NODES // NT
NHALF = (320, 305)
EDGES = 20625
BLK = 512
TPB = BLK // P
NBLK = -(-EDGES // BLK)
TILES = NBLK * TPB
FULL_TILES = EDGES // P
TAIL = EDGES - FULL_TILES * P
D = 256
KD = D // P
HID = 512
KH = HID // P
DE = 64
WIN = 64
NWIN = -(-NODES // WIN)
ACC = NODES + WIN - 1
LN_EPS = 1e-5
PAD_DST = -100000
LAG = 5
PAIRS = (NBLK - LAG) // 2
assert LAG + 2 * PAIRS == NBLK and 2 * DE == P


def run_steps(eng, step, last, first=0, pairs=PAIRS):
    for b in range(first, LAG):
        step(b, b // 2, b % 2)
    with eng.Fori(0, pairs) as i:
        step(2 * i + LAG, i + LAG // 2, LAG % 2)
        step(2 * i + LAG + 1, i + (LAG + 1) // 2, (LAG + 1) % 2)
    for b in range(LAG + 2 * pairs, last + 1):
        step(b, b // 2, b % 2)


def at_least(b, k):
    return b >= k if isinstance(b, int) else True


def inside(b):
    return 0 <= b < NBLK if isinstance(b, int) else True


def gnn_two_layers(nc, x, xT, src, dst, dst_first, efT, eaT, We1, be1, We2, be2, Wn1, bn1, Wn2, bn2, eps,
                   W1, b1, W2, b2, Wg, bg, gamma, beta, out):
    with ExitStack() as ctx:
        def sb(name, shape, dt=F32):
            return ctx.enter_context(nc.sbuf_tensor(name, shape, dt))

        def sem(name):
            return ctx.enter_context(nc.semaphore(name))

        def two(name):
            return [sem(name + "0"), sem(name + "1")]

        xtab = nc.dram_tensor("xtab", [NODES, D], F32, kind="Internal").ap()
        ptab = nc.dram_tensor("ptab", [NODES, 2 * D], F32, kind="Internal").ap()

        hg_sb = sb("hg_sb", [P, 2, TPB, 2 * D])
        flat = hg_sb[:, :, :, :].rearrange("p a t d -> p (a t d)")
        we1_raw = flat[:, 0:1024].rearrange("p (k n) -> p k n", k=KD)
        we2_raw = flat[:, 1024:2048].rearrange("p (k n) -> p k n", k=KH)
        hf = flat[:, 2048:3072].rearrange("p (m e) -> p m e", m=2)
        w2_raw = flat[:, 3072:3584].rearrange("p (k n) -> p k n", k=KD)
        wp_raw = flat[:, 3584:4096]

        we1 = [sb(f"we1_{n}", [P, KD, HID], F32R) for n in "hl"]
        we2 = [sb(f"we2_{n}", [P, KH, D], F32R) for n in "hl"]
        w2 = [sb(f"w2_{n}", [P, KD, D], F32R) for n in "hl"]
        wp_hi = sb("wp_hi", [P, 2 * D], F32R)
        wp = sb("wp", [P, 2 * D], F32R)
        wx = sb("wx", [P, KD, 2 * D])
        wn1 = sb("wn1", [P, KD, HID])
        wn2 = sb("wn2", [P, KH, D])
        b2pad_raw = sb("b2pad_raw", [P, D])
        b2hi = sb("b2hi", [P, D], F32R)
        b2r = sb("b2r", [P, D], F32R)
        ones_r = sb("ones_r", [P, P], F32R)
        be1c = sb("be1c", [P, KH])
        bn1c = sb("bn1c", [P, KH])
        be2b = sb("be2b", [P, D])
        bn2b = sb("bn2b", [NP, D])
        bpb = sb("bpb", [NP, 2 * D])
        ones1 = sb("ones1", [1, P])
        ones_f = sb("ones_f", [P, P])
        gamma_b = sb("gamma_b", [P, D])
        beta_b = sb("beta_b", [P, D])
        epsp1 = sb("epsp1", [P, 1])
        ident = sb("ident", [P, P])

        xn = sb("xn", [NP, NT, D])
        acc = sb("acc", [P, KD, ACC])
        hT = sb("hT", [P, KD, NODES])
        yn = sb("yn", [NP, NT, D])
        xb2 = yn
        x1 = sb("x1", [NP, NT, D])
        stats = sb("stats", [NP, NT, 6])
        mv = sb("mv", [NP, NT, 2])
        sd = sb("sd", [NP, NT])
        rstd = sb("rstd", [NP, NT])

        src_all = sb("src_all", [P, TILES], I32)
        src_slot = sb("src_slot", [P, 2, TPB], I32)
        dst_i = sb("dst_i", [P, TILES], I32)
        dst_f = sb("dst_f", [P, TILES])
        dst_r = sb("dst_r", [P, TILES])
        first_i = sb("first_i", [1, NBLK], I32)
        first_f = sb("first_f", [1, NBLK])
        clamp = sb("clamp", [P, TILES])
        off = sb("off", [P, 1])
        off_i = sb("off_i", [1, 1], I32)
        iota = sb("iota", [P, NWIN * WIN])

        raw = sb("raw", [P, 2, KD, BLK])
        xh = sb("xh", [P, 2, KD, BLK], F32R)
        xl = sb("xl", [P, 2, KD, BLK], F32R)
        hh = sb("hh", [P, 2, KH, BLK], F32R)
        hl = sb("hl", [P, 2, KH, BLK], F32R)
        xg = sb("xg", [P, 2, TPB, 2 * D])
        mf_gate = sb("mf_gate", [P, 2, 2, TPB, D])
        mf = mf_gate[:, 0, :, :, :]
        gate = mf_gate[:, 1, :, :, :]
        mp = [sb(f"mp_{n}", [P, 2, TPB, D], BF16) for n in range(3)]
        r1T = xg[:, :, :, :].rearrange("p a t d -> p (a t d)")[:, 0:KH * NODES].rearrange("p (k n) -> p k n", k=KH)
        pt = mf_gate[0:NP, :, :, :, :].rearrange("p g a t d -> p (g a t d)")[:, 0:NT * 2 * D].rearrange("p (t d) -> p t d", t=NT)
        onehot = sb("onehot", [P, 2, TPB, WIN], BF16)
        onehot_f = sb("onehot_f", [P, 2, TPB, WIN])

        bank = [ctx.enter_context(nc.psum_tensor(f"bank{i}", [P, 512], F32)) for i in range(8)]

        s_we1, s_we2, s_w2, s_wp = sem("s_we1"), sem("s_we2"), sem("s_w2"), sem("s_wp")
        s_b2, s_small, s_x, s_idx, s_src, s_nodew = sem("s_b2"), sem("s_small"), sem("s_x"), sem("s_idx"), sem("s_src"), sem("s_nodew")
        s_xtab, s_ptab, s_out = sem("s_xtab"), sem("s_ptab"), sem("s_out")
        pool_const, dve_const = sem("pool_const"), sem("dve_const")
        hi_w, lo_w = sem("hi_w"), sem("lo_w")
        xb2_ready, prep, base_ps, off_ps, flag_ready = sem("xb2_ready"), sem("prep"), sem("base_ps"), sem("off_ps"), sem("flag_ready")
        L = [{n: sem(f"{n}_l{k}") for n in
              ("hi_done", "lo_done", "h_mm", "h_evac", "hl_done", "z_mm", "window_mm", "m_done", "mp0_done", "rest_done", "mp1_done", "mp2_done",
               "slot_done", "oh_done", "acc_done", "u_mm", "hg_done", "t_mm", "rh_done", "rl_done",
               "gate_done", "summed", "all_summed")} for k in range(2)]
        loaded = [two("loaded_l0_"), two("loaded_l1_")]
        gathered = [two("gathered_l0_"), two("gathered_l1_")]
        acc_zero, h0_ready, n1_mm, r1_done, n2_mm, y_done, ln, sq, x1_done = (sem(n) for n in (
            "acc_zero", "h0_ready", "n1_mm", "r1_done", "n2_mm", "y_done", "ln", "sq", "x1_done"))
        lnstep, xbn2_done = sem("lnstep"), sem("xbn2_done")
        b2z = sem("b2z")
        xt_mm, xt_done, p_mm, p_done, fin_mm, fin_done, res_done = (sem(n) for n in (
            "xt_mm", "xt_done", "p_mm", "p_done", "fin_mm", "fin_done", "res_done"))

        block = ctx.enter_context(nc.Block())

        def rows(w, n):
            return w.rearrange("(k p) n -> p k n", p=P)

        @block.sync
        def _(sp):
            def load0(b, half, q):
                if at_least(b, 2):
                    sp.wait_ge(L[0]["lo_done"], b - 1)
                sp.dma_start(raw[:, q, :, :], efT[:, :, bass.ds(b * BLK, BLK)]).then_inc(loaded[0][q], 16)

            def load1(b, half, q):
                if at_least(b, 2):
                    sp.wait_ge(L[1]["lo_done"], b - 1)
                else:
                    sp.wait_ge(L[0]["lo_done"], NBLK)
                sp.dma_start(raw[0:DE, q, 0, :], eaT[:, bass.ds(b * BLK, BLK)]).then_inc(loaded[1][q], 16)
                sp.dma_start(raw[DE:P, q, 0, :], eaT[:, bass.ds(b * BLK, BLK)]).then_inc(loaded[1][q], 16)

            load0(0, 0, 0)
            sp.dma_start(we1_raw[:, :, :], rows(We1, HID)).then_inc(s_we1, 16)
            sp.dma_start(we2_raw[:, :, :], rows(We2, D)).then_inc(s_we2, 16)
            sp.dma_start(xn[:, :, :], x.rearrange("(t p) d -> p t d", p=NP)).then_inc(s_x, 16)
            sp.dma_start(be2b[:, :], be2.partition_broadcast(P)).then_inc(s_x, 16)
            load0(1, 0, 1)
            sp.wait_ge(xb2_ready, NT)
            sp.dma_start(xtab.rearrange("(t p) d -> p t d", p=NP), xb2[:, :, :]).then_inc(s_xtab, 16)
            sp.dma_start(w2_raw[:, :, :], rows(W2, D)).then_inc(s_w2, 16)
            for h in range(2):
                for g, w in enumerate((W1, Wg)):
                    sp.dma_start(wp_raw[h * DE:(h + 1) * DE, g * D:(g + 1) * D], w[D:D + DE, :]).then_inc(s_wp, 16)
            sp.wait_ge(pool_const, 2)
            for row in (0, 32):
                sp.dma_start(b2pad_raw[row:row + 1, :], b2).then_inc(s_b2, 16)
            for g, w in enumerate((W1, Wg)):
                sp.dma_start(wx[:, :, g * D:(g + 1) * D], rows(w[0:D, :], D)).then_inc(s_nodew, 16)
            sp.dma_start(wn1[:, :, :], rows(Wn1, HID)).then_inc(s_nodew, 16)
            sp.dma_start(wn2[:, :, :], rows(Wn2, D)).then_inc(s_nodew, 16)
            sp.dma_start(hT[:, :, :], rows(xT, NODES)).then_inc(s_nodew, 16)
            sp.dma_start(bn2b[:, :], bn2.partition_broadcast(NP)).then_inc(s_nodew, 16)
            sp.dma_start(bpb[:, 0:D], b1.partition_broadcast(NP)).then_inc(s_nodew, 16)
            sp.dma_start(bpb[:, D:2 * D], bg.partition_broadcast(NP)).then_inc(s_nodew, 16)
            sp.dma_start(gamma_b[:, :], gamma.partition_broadcast(P)).then_inc(s_nodew, 16)
            sp.dma_start(beta_b[:, :], beta.partition_broadcast(P)).then_inc(s_nodew, 16)

            run_steps(sp, load0, NBLK - 1, first=2)

            load1(0, 0, 0)
            load1(1, 0, 1)
            sp.wait_ge(p_done, NT)
            sp.dma_start(ptab.rearrange("(t p) d -> p t d", p=NP), pt[:, :, :]).then_inc(s_ptab, 16)
            run_steps(sp, load1, NBLK - 1, first=2)

            sp.wait_ge(res_done, NT)
            sp.dma_start(out.rearrange("(t p) d -> p t d", p=NP), yn[:, :, :]).then_inc(s_out, 16)
            sp.wait_ge(s_out, 16)

        @block.gpsimd
        def _(pool):
            pool.dma_start(first_i[:, :], dst_first).then_inc(s_idx, 16)
            pool.dma_start(dst_i[:, :], dst).then_inc(s_idx, 16)
            pool.dma_start(src_all[:, :], src).then_inc(s_src, 16)
            nc.gpsimd.iota(iota[:, :], [[1, NWIN * WIN]], base=0, channel_multiplier=0,
                           allow_small_or_imprecise_dtypes=True).then_inc(pool_const, 1)
            nc.gpsimd.memset(b2pad_raw[:, :], 0.0).then_inc(pool_const, 1)
            nc.gpsimd.memset(ident[:, :], 0.0).then_inc(pool_const, 1)
            pool.wait_ge(pool_const, 3)
            nc.gpsimd.affine_select(out=ident[:, :], in_=ident[:, :], compare_op=ALU.not_equal, fill=1.0, base=0,
                                    pattern=[[-1, P]], channel_multiplier=1).then_inc(pool_const, 1)

            def slots(k, b, q):
                nc.gpsimd.tensor_copy(src_slot[:, q, :], src_all[:, bass.ds(b * TPB, TPB)]).then_inc(L[k]["slot_done"], 1)

            def gather(k, b, half, q, table, width):
                if at_least(b, 1):
                    pool.wait_ge(gathered[k][1 - q], 64 * (half + (q == 1)))
                if at_least(b, 2):
                    pool.wait_ge(L[k]["m_done" if k == 0 else "hg_done"], (b - 1) * (2 if k == 0 else TPB))
                pool.wait_ge(L[k]["slot_done"], b + 1)
                if not isinstance(b, int) or b + 1 < NBLK:
                    slots(k, b + 1, 1 - q)
                else:
                    slots(k, 0, 1 - q)
                for t in range(TPB):
                    nc.gpsimd.indirect_dma_start(
                        xg[:, q, t, 0:width], None, table,
                        bass.IndirectOffsetOnAxis(ap=src_slot[:, q, t:t + 1].bitcast(U32), axis=0),
                    ).then_inc(gathered[k][q], 16)

            def lo(k, b, q, n):
                pool.wait_ge(L[k]["hi_done"], b + 1)
                if at_least(b, 2):
                    pool.wait_ge(L[k]["h_mm" if k == 0 else "u_mm"], (b - 1) * TPB)
                elif k == 1:
                    pool.wait_ge(L[0]["h_mm"], NBLK * KH)
                nc.gpsimd.tensor_tensor(xl[:, q, 0:n, :], raw[:, q, 0:n, :], xh[:, q, 0:n, :].bitcast(F32),
                                        ALU.subtract).then_inc(L[k]["lo_done"], 1)

            def step0(b, half, q):
                gather(0, b, half, q, xtab, D)
                if not isinstance(b, int) or b + 2 < NBLK:
                    lo(0, b + 2, q, KD)

            pool.wait_ge(s_src, 16)
            slots(0, 0, 0)
            lo(0, 0, 0, KD)
            lo(0, 1, 1, KD)
            pool.wait_ge(s_xtab, 16)
            run_steps(pool, step0, NBLK - 1, pairs=PAIRS - 1)

            def step1(b, half, q):
                if not isinstance(b, int) or b + 1 < NBLK:
                    gather(1, b + 1, half + (q == 1), 1 - q, ptab, 2 * D)
                    lo(1, b + 1, 1 - q, 1)

            pool.wait_ge(gathered[0][0], 64 * ((NBLK + 1) // 2))
            pool.wait_ge(L[0]["slot_done"], NBLK + 1)
            slots(1, 0, 0)
            lo(1, 0, 0, 1)
            pool.wait_ge(L[0]["m_done"], 2 * NBLK)
            pool.wait_ge(s_ptab, 16)
            gather(1, 0, 0, 0, ptab, 2 * D)
            run_steps(pool, step1, NBLK - 1, pairs=PAIRS - 1)

        @block.scalar
        def _(act):

            def hi(k, b, half, q, n):
                act.wait_ge(loaded[k][q], (16 if k == 0 else 32) * (half + 1))
                if at_least(b, 2):
                    act.wait_ge(L[k]["h_mm" if k == 0 else "u_mm"], (b - 1) * TPB)
                    act.wait_ge(L[k]["lo_done"], b - 1)
                elif k == 1:
                    act.wait_ge(L[0]["h_mm"], NBLK * KH)
                nc.scalar.activation(xh[:, q, 0:n, :], raw[:, q, 0:n, :], ACT.Copy).then_inc(L[k]["hi_done"], 1)

            hi(0, 0, 0, 0, KD)
            act.wait_ge(s_we1, 16)
            nc.scalar.activation(we1[0][:, :, :], we1_raw[:, :, :], ACT.Copy).then_inc(hi_w, 1)
            act.dma_start(be1c[:, :], be1).then_inc(s_small, 16)
            act.dma_start(bn1c[:, :], bn1).then_inc(s_small, 16)
            act.dma_start(epsp1[:, :], eps.partition_broadcast(P)).then_inc(s_small, 16)
            act.wait_ge(s_we2, 16)
            nc.scalar.activation(we2[0][:, :, :], we2_raw[:, :, :], ACT.Copy).then_inc(hi_w, 1)
            hi(0, 1, 0, 1, KD)
            act.wait_ge(s_small, 48)

            def h_chunk(b, q, m):
                n = TPB * b + m
                act.wait_ge(L[0]["h_mm"], n + 1)
                if at_least(b, 2):
                    act.wait_ge(L[0]["z_mm"], 2 * (b - 1))
                nc.scalar.activation(hh[:, q, m, :], bank[m][:, :], ACT.Relu, bias=be1c[:, m:m + 1])
                if m >= 2 or at_least(b, 1):
                    act.wait_ge(L[0]["hl_done"], n - 1)
                nc.scalar.activation(hf[:, m % 2, :], bank[m][:, :], ACT.Relu, bias=be1c[:, m:m + 1]).then_inc(L[0]["h_evac"], 1)

            def part0(b, q, c):
                tiles = slice(2 * c, 2 * c + 2)
                act.wait_ge(L[0]["m_done"], 2 * b + c + 1)
                if at_least(b, 2):
                    act.wait_ge(L[0]["summed"], b - 1)
                nc.scalar.activation(mp[0][:, q, tiles, :], mf[:, q, tiles, :], ACT.Relu).then_inc(L[0]["mp0_done"], 1)

            def part1(b, q, c):
                tiles = slice(2 * c, 2 * c + 2)
                act.wait_ge(L[0]["rest_done"], 2 * b + c + 1)
                nc.scalar.activation(mp[1][:, q, tiles, :], mf[:, q, tiles, :], ACT.Copy).then_inc(L[0]["mp1_done"], 1)

            def step0(b, half, q):
                if inside(b - 2):
                    part0(b - 2, q, 1)
                if inside(b):
                    h_chunk(b, q, 0)
                if inside(b - 2):
                    part1(b - 2, q, 1)
                if inside(b):
                    for m in range(1, KH):
                        h_chunk(b, q, m)
                if inside(b - 1):
                    part0(b - 1, 1 - q, 0)
                if not isinstance(b, int) or b + 2 < NBLK:
                    hi(0, b + 2, half + 1, q, KD)
                if inside(b - 1):
                    part1(b - 1, 1 - q, 0)

            run_steps(act, step0, NBLK + 1, pairs=PAIRS - 1)

            act.wait_ge(s_w2, 16)
            nc.scalar.activation(w2[0][:, :, :], w2_raw[:, :, :], ACT.Copy).then_inc(hi_w, 1)
            act.wait_ge(s_wp, 64)
            nc.scalar.activation(wp_hi[:, :], wp_raw[:, :], ACT.Copy).then_inc(hi_w, 1)
            act.wait_ge(s_b2, 32)
            nc.scalar.activation(b2hi[:, :], b2pad_raw[:, :], ACT.Copy).then_inc(hi_w, 1)
            hi(1, 0, 0, 0, 1)

            for m in range(KH):
                act.wait_ge(n1_mm, m + 1)
                nc.scalar.activation(r1T[:, m, 0:NHALF[0]], bank[2 * (m % 2)][:, 0:NHALF[0]], ACT.Relu, bias=bn1c[:, m:m + 1]).then_inc(r1_done, 1)
                nc.scalar.activation(r1T[:, m, NHALF[0]:NODES], bank[2 * (m % 2) + 1][:, 0:NHALF[1]], ACT.Relu, bias=bn1c[:, m:m + 1]).then_inc(r1_done, 1)

            def roots(k):
                act.wait_ge(ln, k)
                nc.scalar.activation(sd[:, :], mv[:, :, 1], ACT.Sqrt).then_inc(sq, 1)

            roots(1)

            def gates(b, half, q):
                act.wait_ge(L[1]["hg_done"], TPB * (b + 1))
                if at_least(b, 2):
                    act.wait_ge(L[1]["m_done"], 2 * (b - 1))
                nc.scalar.activation(gate[:, q, :, :], hg_sb[:, q, :, D:2 * D], ACT.Sigmoid).then_inc(L[1]["gate_done"], 1)

            def rh(b, q):
                for k in range(KD):
                    act.wait_ge(L[1]["t_mm"], b + 1)
                    if at_least(b, 2):
                        act.wait_ge(L[1]["z_mm"], 2 * (b - 1))
                    nc.scalar.activation(hh[:, q, k, :], bank[2 + k][:, :], ACT.Relu).then_inc(L[1]["rh_done"], 1)

            def step1(b, half, q):
                if inside(b - 1):
                    rh(b - 1, 1 - q)
                if not isinstance(b, int) or b + 1 < NBLK:
                    hi(1, b + 1, half + (q == 1), 1 - q, 1)
                if inside(b - 1):
                    gates(b - 1, half, 1 - q)

            run_steps(act, step1, NBLK, pairs=PAIRS - 1)
            roots(2)
            roots(3)

        @block.tensor
        def _(pe):
            pe.wait_ge(prep, 2)
            nc.tensor.matmul(bank[6][:, 0:NBLK], ones1[0:1, :], first_f[0:1, :], start=True, stop=True).then_inc(base_ps, 1)
            def scatter(k, b, q, gen):
                S = L[k]
                if k == 0:
                    pe.wait_ge(S["mp2_done"], 2 * b + 2)
                    parts, hot = mp, onehot
                else:
                    pe.wait_ge(S["m_done"], 2 * b + 2)
                    parts, hot = (mf,), onehot_f
                for w in range(NWIN if gen else 1):
                    n = NWIN * b + w if gen else b
                    u = w % 2 if gen else q
                    pe.wait_ge(S["oh_done"], n + 1)
                    if at_least(b, 2) or w >= 2 or (gen and at_least(b, 1)):
                        pe.wait_ge(S["acc_done"], n - 1)
                    for f in range(KD):
                        for t in range(TPB):
                            for part, m in enumerate(parts):
                                mm = nc.tensor.matmul(bank[6 + u][:, f * WIN:(f + 1) * WIN], m[:, q, t, f * P:(f + 1) * P],
                                                      hot[:, u, t, :], start=(t == 0 and part == 0),
                                                      stop=(t == TPB - 1 and part == len(parts) - 1))
                    mm.then_inc(S["summed" if w == (NWIN - 1 if gen else 0) else "window_mm"], 1)

            def h_mm(b, q):
                pe.wait_ge(L[0]["hi_done"], b + 1)
                pe.wait_ge(L[0]["lo_done"], b + 1)
                for m in range(KH):
                    if at_least(b, 1):
                        pe.wait_ge(L[0]["h_evac"], TPB * (b - 1) + m + 1)
                    passes = [(k, w, v) for k in range(KD) for w, v in ((0, xh), (0, xl), (1, xh))]
                    for n, (k, w, v) in enumerate(passes):
                        mm = nc.tensor.matmul(bank[m][:, :], we1[w][:, k, m * P:(m + 1) * P], v[:, q, k, :],
                                              start=(n == 0), stop=(n == len(passes) - 1))
                    mm.then_inc(L[0]["h_mm"], 1)

            def z_mm(b, q):
                pe.wait_ge(L[0]["hl_done"], TPB * (b + 1))
                for c in range(2):
                    if at_least(b, 1):
                        pe.wait_ge(L[0]["m_done"], 2 * (b - 1) + c + 1)
                    for t in (2 * c, 2 * c + 1):
                        passes = [(k, w, v) for k in range(KH) for v, w in ((hh, 0), (hh, 1), (hl, 0))]
                        for n, (k, w, v) in enumerate(passes):
                            mm = nc.tensor.matmul(bank[4 + c][:, (t % 2) * D:(t % 2 + 1) * D], v[:, q, k, t * P:(t + 1) * P],
                                                  we2[w][:, k, :], start=(n == 0), stop=(n == len(passes) - 1))
                    mm.then_inc(L[0]["z_mm"], 1)

            def layer0(gen):
                def step(b, half, q):
                    if inside(b):
                        h_mm(b, q)
                    if inside(b - 1):
                        z_mm(b - 1, 1 - q)
                    if inside(b - 2):
                        scatter(0, b - 2, q, gen)
                run_steps(pe, step, NBLK + 1, first=1)

            pe.wait_ge(hi_w, 1)
            pe.wait_ge(lo_w, 1)
            h_mm(0, 0)
            pe.wait_ge(prep, 8)
            nc.tensor.matmul(bank[7][:, 0:1], ones_f[:, :], off[:, :], start=True, stop=True).then_inc(off_ps, 1)
            pe.wait_ge(flag_ready, 1)
            outside = pe.value_load(off_i[0:1, 0:1], min_val=0, max_val=1)

            pe.wait_ge(hi_w, 2)
            pe.wait_ge(lo_w, 2)
            with pe.If(outside < 1):
                layer0(False)
            with pe.Else():
                layer0(True)

            pe.wait_ge(s_nodew, 16 * 10)
            pe.wait_ge(h0_ready, 1)
            starts = (0, NHALF[0])
            for m in range(KH):
                if m >= 2:
                    pe.wait_ge(r1_done, 2 * (m - 1))
                for c in range(2):
                    for k in range(KD):
                        mm = nc.tensor.matmul(bank[2 * (m % 2) + c][:, 0:NHALF[c]], wn1[:, k, m * P:(m + 1) * P],
                                              hT[:, k, starts[c]:starts[c] + NHALF[c]], start=(k == 0), stop=(k == KD - 1))
                mm.then_inc(n1_mm, 1)
            pe.wait_ge(r1_done, 2 * KH)
            for t in range(NT):
                if t >= 2:
                    pe.wait_ge(y_done, t - 1)
                for k in range(KH):
                    mm = nc.tensor.matmul(bank[4 + t % 2][0:NP, 0:D], r1T[:, k, t * NP:(t + 1) * NP], wn2[:, k, :],
                                          start=(k == 0), stop=(k == KH - 1))
                mm.then_inc(n2_mm, 1)
            for t in range(NT):
                pe.wait_ge(x1_done, t + 1)
                if t >= 2:
                    pe.wait_ge(xt_done, t - 1)
                for k in range(KD):
                    mm = nc.tensor.transpose(bank[t % 2][:, k * P:k * P + NP], x1[:, t, k * P:(k + 1) * P], ident[0:NP, 0:NP])
                mm.then_inc(xt_mm, 1)
            for t in range(NT):
                pe.wait_ge(xt_done, t + 1)
                if t >= 2:
                    pe.wait_ge(p_done, t - 1)
                for k in range(KD):
                    mm = nc.tensor.matmul(bank[2 + t % 2][0:NP, :], hT[:, k, t * NP:(t + 1) * NP], wx[:, k, :],
                                          start=(k == 0), stop=(k == KD - 1))
                mm.then_inc(p_mm, 1)

            def u_tile(b, q, t):
                if t == 0:
                    pe.wait_ge(L[1]["hi_done"], b + 1)
                    pe.wait_ge(L[1]["lo_done"], b + 1)
                if t >= 2 or at_least(b, 1):
                    pe.wait_ge(L[1]["hg_done"], TPB * b + t - 1)
                for n, v in enumerate((xh, xl)):
                    mm = nc.tensor.matmul(bank[t % 2][:, :], v[:, q, 0, t * P:(t + 1) * P], wp[:, :], start=(n == 0), stop=(n == 1))
                mm.then_inc(L[1]["u_mm"], 1)

            def c_tile(b, q, t):
                c = t // 2
                if t == 0:
                    pe.wait_ge(L[1]["rl_done"], KD * (b + 1))
                if t % 2 == 0 and at_least(b, 1):
                    pe.wait_ge(L[1]["m_done"], 2 * (b - 1) + c + 1)
                passes = [(ones_r[:, :], b2r[:, :])]
                passes += [(v[:, q, k, t * P:(t + 1) * P], w2[w][:, k, :]) for k in range(KD) for v, w in ((hh, 0), (hh, 1), (hl, 0))]
                for n, (lhs, rhs) in enumerate(passes):
                    mm = nc.tensor.matmul(bank[4 + c][:, (t % 2) * D:(t % 2 + 1) * D], lhs, rhs, start=(n == 0), stop=(n == len(passes) - 1))
                if t % 2:
                    mm.then_inc(L[1]["z_mm"], 1)

            def t_mm(b, q):
                pe.wait_ge(L[1]["hg_done"], TPB * (b + 1))
                if at_least(b, 1):
                    pe.wait_ge(L[1]["rl_done"], KD * b)
                for k in range(KD):
                    for t in range(TPB):
                        mm = nc.tensor.transpose(bank[2 + k][:, t * P:(t + 1) * P], hg_sb[:, q, t, k * P:(k + 1) * P], ident[:, :])
                mm.then_inc(L[1]["t_mm"], 1)

            def layer1(gen):
                def step(b, half, q):
                    if inside(b - 1):
                        t_mm(b - 1, 1 - q)
                    for t in range(TPB):
                        if inside(b):
                            u_tile(b, q, t)
                        if inside(b - 2):
                            c_tile(b - 2, q, t)
                    if inside(b - 3):
                        scatter(1, b - 3, 1 - q, gen)
                run_steps(pe, step, NBLK + 2)

            pe.wait_ge(hi_w, 5)
            pe.wait_ge(lo_w, 5)
            with pe.If(outside < 1):
                layer1(False)
            with pe.Else():
                layer1(True)

            pe.wait_ge(L[1]["all_summed"], 1)
            for t in range(NT):
                if t >= 2:
                    pe.wait_ge(fin_done, t - 1)
                for k in range(KD):
                    mm = nc.tensor.transpose(bank[t % 2][0:NP, k * P:(k + 1) * P], acc[:, k, t * NP:(t + 1) * NP], ident[:, :])
                mm.then_inc(fin_mm, 1)

        @block.vector
        def _(dve):
            nprep = [0]

            def p_step(ins):
                nprep[0] += 1
                ins.then_inc(prep, 1)
                dve.wait_ge(prep, nprep[0])

            p_step(nc.vector.memset(ones1[:, :], 1.0))
            dve.wait_ge(s_idx, 32)
            p_step(nc.vector.tensor_copy(first_f[:, :], first_i[:, :]))
            dve.wait_ge(hi_w, 1)
            nc.vector.tensor_tensor(we1[1][:, :, :], we1_raw[:, :, :],
                                    we1[0][:, :, :].bitcast(F32), ALU.subtract).then_inc(lo_w, 1)
            nc.vector.memset(ones_f[:, :], 1.0)
            dve.wait_ge(s_x, 32)
            for t in range(NT):
                nc.vector.tensor_tensor(xb2[:, t, :], xn[:, t, :], be2b[0:NP, :], ALU.add).then_inc(xb2_ready, 1)
            dve.wait_ge(hi_w, 2)
            nc.vector.tensor_tensor(we2[1][:, :, :], we2_raw[:, :, :], we2[0][:, :, :].bitcast(F32), ALU.subtract).then_inc(lo_w, 1)
            p_step(nc.vector.tensor_copy(dst_f[:, :], dst_i[:, :]))
            dve.wait_ge(base_ps, 1)
            p_step(nc.vector.tensor_tensor(dst_r[:, :].rearrange("p (b t) -> p b t", t=TPB),
                                           dst_f[:, :].rearrange("p (b t) -> p b t", t=TPB),
                                           bank[6][:, 0:NBLK].rearrange("p (b o) -> p b o", o=1).broadcast_to([P, NBLK, TPB]), ALU.subtract))
            p_step(nc.vector.tensor_scalar(clamp[:, :], dst_r[:, :], 0.0, float(WIN - 1), ALU.max, ALU.min))
            p_step(nc.vector.tensor_tensor(clamp[:, :], clamp[:, :], dst_r[:, :], ALU.not_equal))
            p_step(nc.vector.tensor_reduce(off[:, :], clamp[:, 0:FULL_TILES], AX.X, ALU.add))
            p_step(nc.vector.tensor_tensor(off[0:TAIL, :], off[0:TAIL, :], clamp[0:TAIL, FULL_TILES:FULL_TILES + 1], ALU.add))
            nc.vector.memset(acc[:, :, :], 0.0).then_inc(acc_zero, 1)
            def window_multiplied(S, b, gen, w):
                if w == (NWIN - 1 if gen else 0):
                    dve.wait_ge(S["summed"], b + 1)
                else:
                    dve.wait_ge(S["window_mm"], (NWIN - 1) * b + w + 1)

            def one_hot(k, b, q, gen, w=0):
                S = L[k]
                n = NWIN * b + w if gen else b
                u = w % 2 if gen else q
                if gen and w >= 2:
                    window_multiplied(S, b, gen, w - 2)
                elif gen and at_least(b, 1):
                    window_multiplied(S, b - 1, gen, NWIN - 2 + w)
                elif at_least(b, 2) and not gen:
                    window_multiplied(S, b - 2, gen, 0)
                which = dst_f if gen else dst_r
                nc.vector.tensor_tensor(
                    (onehot if k == 0 else onehot_f)[:, u, :, :],
                    iota[:, w * WIN:(w + 1) * WIN].rearrange("p (o w) -> p o w", o=1).broadcast_to([P, TPB, WIN]),
                    which[:, bass.ds(b * TPB, TPB)].rearrange("p (t o) -> p t o", o=1).broadcast_to([P, TPB, WIN]),
                    ALU.is_equal).then_inc(S["oh_done"], 1)

            def add_window(k, b, q, gen, w=0):
                S = L[k]
                n = NWIN * b + w if gen else b
                u = w % 2 if gen else q
                window_multiplied(S, b, gen, w)
                if w >= 1 or at_least(b, 1):
                    dve.wait_ge(S["acc_done"], n)
                else:
                    dve.wait_ge(acc_zero, k + 1)
                first = w * WIN if gen else dve.value_load(first_i[0:1, bass.ds(b, 1)], min_val=0, max_val=NODES - 1)
                width = min(WIN, ACC - w * WIN) if gen else WIN
                where = acc[:, :, first:first + width] if gen else acc[:, :, bass.ds(first, WIN)]
                nc.vector.tensor_tensor(
                    where, where, bank[6 + u][:, 0:KD * WIN].rearrange("p (f w) -> p f w", f=KD)[:, :, 0:width],
                    ALU.add).then_inc(S["acc_done"], 1)

            def scatter_all(k, b, q):
                for w in range(NWIN):
                    one_hot(k, b, q, True, w)
                    add_window(k, b, q, True, w)

            def hl_chunk(b, q, m):
                n = TPB * b + m
                dve.wait_ge(L[0]["h_evac"], n + 1)
                if at_least(b, 2):
                    dve.wait_ge(L[0]["z_mm"], 2 * (b - 1))
                nc.vector.tensor_tensor(hl[:, q, m, :], hf[:, m % 2, :], hh[:, q, m, :].bitcast(F32), ALU.subtract).then_inc(L[0]["hl_done"], 1)

            def m0(b, half, q, c):
                dve.wait_ge(L[0]["z_mm"], 2 * b + c + 1)
                if c == 0:
                    dve.wait_ge(gathered[0][q], 64 * (half + 1))
                nc.vector.tensor_tensor(mf[:, q, 2 * c:2 * c + 2, :], bank[4 + c][:, :].rearrange("p (t d) -> p t d", t=2),
                                        xg[:, q, 2 * c:2 * c + 2, 0:D], ALU.add).then_inc(L[0]["m_done"], 1)

            def rest0(b, q, c):
                tiles = slice(2 * c, 2 * c + 2)
                dve.wait_ge(L[0]["mp0_done"], 2 * b + c + 1)
                nc.vector.scalar_tensor_tensor(out=mf[:, q, tiles, :], in0=mf[:, q, tiles, :], scalar=0.0, in1=mp[0][:, q, tiles, :],
                                               op0=ALU.max, op1=ALU.subtract).then_inc(L[0]["rest_done"], 1)

            def part2(b, q, c):
                tiles = slice(2 * c, 2 * c + 2)
                dve.wait_ge(L[0]["mp1_done"], 2 * b + c + 1)
                nc.vector.tensor_tensor(mp[2][:, q, tiles, :], mf[:, q, tiles, :], mp[1][:, q, tiles, :],
                                        ALU.subtract).then_inc(L[0]["mp2_done"], 1)

            def layer0(gen):
                def step(b, half, q):
                    if inside(b - 2):
                        rest0(b - 2, q, 1)
                        if not gen:
                            one_hot(0, b - 2, q, gen)
                    if inside(b):
                        hl_chunk(b, q, 0)
                    if inside(b - 2):
                        part2(b - 2, q, 1)
                    if inside(b):
                        for m in range(1, KH):
                            hl_chunk(b, q, m)
                    if inside(b - 1):
                        hb = half - (q == 0)
                        m0(b - 1, hb, 1 - q, 0)
                        rest0(b - 1, 1 - q, 0)
                        m0(b - 1, hb, 1 - q, 1)
                        part2(b - 1, 1 - q, 0)
                    if inside(b - 2):
                        if gen:
                            scatter_all(0, b - 2, q)
                        else:
                            add_window(0, b - 2, q, gen)
                run_steps(dve, step, NBLK + 1, first=1)

            for m in range(KH):
                hl_chunk(0, 0, m)
            dve.wait_ge(off_ps, 1)
            nc.vector.tensor_scalar(off_i[:, :], bank[7][0:1, 0:1], 1.0, None, ALU.min).then_inc(flag_ready, 1)
            dve.wait_ge(flag_ready, 1)
            outside = dve.value_load(off_i[0:1, 0:1], min_val=0, max_val=1)
            with dve.If(outside < 1):
                layer0(False)
            with dve.Else():
                layer0(True)

            dve.wait_ge(s_small, 48)
            nc.vector.tensor_scalar(epsp1[:, :], epsp1[:, :], 1.0, None, ALU.add).then_inc(dve_const, 1)
            dve.wait_ge(dve_const, 1)
            dve.wait_ge(s_nodew, 16 * 10)
            nc.vector.scalar_tensor_tensor(out=hT[:, :, :], in0=hT[:, :, :], scalar=epsp1[:, 0:1], in1=acc[:, :, 0:NODES],
                                           op0=ALU.mult, op1=ALU.add).then_inc(h0_ready, 1)
            dve.wait_ge(h0_ready, 1)
            nc.vector.memset(acc[:, :, :], 0.0).then_inc(acc_zero, 1)
            for t in range(NT):
                nc.vector.tensor_tensor(xn[:, t, :], xn[:, t, :], bn2b[:, :], ALU.add).then_inc(xbn2_done, 1)
            dve.wait_ge(hi_w, 5)
            nc.vector.tensor_tensor(w2[1][:, :, :], w2_raw[:, :, :], w2[0][:, :, :].bitcast(F32), ALU.subtract).then_inc(lo_w, 1)
            nc.vector.tensor_copy(wp[0:DE, :], wp_hi[0:DE, :].bitcast(F32))
            nc.vector.tensor_tensor(wp[DE:P, :], wp_raw[DE:P, :], wp_hi[DE:P, :].bitcast(F32), ALU.subtract).then_inc(lo_w, 1)
            nc.vector.tensor_copy(ones_r[:, :], ones_f[:, :])
            nc.vector.memset(b2r[:, :].bitcast(F32), 0.0).then_inc(b2z, 1)
            dve.wait_ge(b2z, 1)
            nc.vector.tensor_copy(b2r[0:32, :], b2hi[0:32, :].bitcast(F32))
            nc.vector.tensor_tensor(b2r[32:64, :], b2pad_raw[32:64, :], b2hi[32:64, :].bitcast(F32), ALU.subtract).then_inc(lo_w, 1)

            nln = [0]

            def link(ins):
                nln[0] += 1
                ins.then_inc(lnstep, 1)
                dve.wait_ge(lnstep, nln[0])

            def moments(k):
                for t in range(NT):
                    ins = nc.vector.bn_stats(stats[:, t, :], yn[:, t, :])
                link(ins)
                for t in range(NT):
                    ins = nc.vector.bn_aggr(mv[:, t, :], stats[:, t, :])
                link(ins)
                nc.vector.tensor_scalar(mv[:, :, 1], mv[:, :, 1], LN_EPS, None, ALU.add).then_inc(ln, 1)
                dve.wait_ge(sq, k)
                link(nc.vector.reciprocal(rstd[:, :], sd[:, :]))

            dve.wait_ge(xbn2_done, NT)
            for t in range(NT):
                dve.wait_ge(n2_mm, t + 1)
                nc.vector.tensor_tensor(yn[:, t, :], bank[4 + t % 2][0:NP, 0:D], xn[:, t, :], ALU.add).then_inc(y_done, 1)
            dve.wait_ge(y_done, NT)
            moments(1)
            for t in range(NT):
                nc.vector.tensor_scalar(x1[:, t, :], yn[:, t, :], mv[:, t, 0:1], rstd[:, t:t + 1], ALU.subtract, ALU.mult).then_inc(x1_done, 1)
            for t in range(NT):
                dve.wait_ge(xt_mm, t + 1)
                nc.vector.tensor_copy(hT[:, :, t * NP:(t + 1) * NP],
                                      bank[t % 2][:, 0:KD * P].rearrange("p (k n) -> p k n", k=KD)[:, :, 0:NP]).then_inc(xt_done, 1)
            for t in range(NT):
                dve.wait_ge(p_mm, t + 1)
                nc.vector.tensor_tensor(pt[:, t, :], bank[2 + t % 2][0:NP, :], bpb[:, :], ALU.add).then_inc(p_done, 1)

            def hg(b, half, q, t):
                dve.wait_ge(L[1]["u_mm"], TPB * b + t + 1)
                if t == 0:
                    dve.wait_ge(gathered[1][q], 64 * (half + 1))
                    if at_least(b, 2):
                        dve.wait_ge(L[1]["t_mm"], b - 1)
                        dve.wait_ge(L[1]["gate_done"], b - 1)
                nc.vector.tensor_tensor(hg_sb[:, q, t, :], bank[t % 2][:, :], xg[:, q, t, :], ALU.add).then_inc(L[1]["hg_done"], 1)

            def rl(b, q):
                for k in range(KD):
                    dve.wait_ge(L[1]["rh_done"], KD * b + k + 1)
                    if at_least(b, 2):
                        dve.wait_ge(L[1]["z_mm"], 2 * (b - 1))
                    nc.vector.scalar_tensor_tensor(out=hl[:, q, k, :], in0=bank[2 + k][:, :], scalar=0.0, in1=hh[:, q, k, :].bitcast(F32),
                                                   op0=ALU.max, op1=ALU.subtract).then_inc(L[1]["rl_done"], 1)

            def m1(b, q, c):
                dve.wait_ge(L[1]["z_mm"], 2 * b + c + 1)
                dve.wait_ge(L[1]["gate_done"], b + 1)
                if at_least(b, 2):
                    dve.wait_ge(L[1]["summed"], b - 1)
                nc.vector.tensor_tensor(mf[:, q, 2 * c:2 * c + 2, :], bank[4 + c][:, :].rearrange("p (t d) -> p t d", t=2),
                                        gate[:, q, 2 * c:2 * c + 2, :], ALU.mult).then_inc(L[1]["m_done"], 1)

            def layer1(gen):
                def step(b, half, q):
                    if inside(b):
                        hg(b, half, q, 0)
                    if inside(b - 4) and not gen:
                        add_window(1, b - 4, q, gen)
                    if inside(b):
                        hg(b, half, q, 1)
                    if inside(b - 1):
                        rl(b - 1, 1 - q)
                    if inside(b - 2):
                        m1(b - 2, q, 0)
                    if inside(b):
                        hg(b, half, q, 2)
                        hg(b, half, q, 3)
                    if inside(b - 2):
                        m1(b - 2, q, 1)
                        if not gen:
                            one_hot(1, b - 2, q, gen)
                    if inside(b - 3) and gen:
                        scatter_all(1, b - 3, 1 - q)
                run_steps(dve, step, NBLK + 3)

            with dve.If(outside < 1):
                layer1(False)
            with dve.Else():
                layer1(True)
            nc.vector.memset(clamp[:, :], 0.0).then_inc(L[1]["all_summed"], 1)

            for t in range(NT):
                dve.wait_ge(fin_mm, t + 1)
                nc.vector.tensor_tensor(yn[:, t, :], bank[t % 2][0:NP, 0:D], x1[:, t, :], ALU.add).then_inc(fin_done, 1)
            dve.wait_ge(fin_done, NT)
            moments(2)
            for t in range(NT):
                link(nc.vector.tensor_scalar(yn[:, t, :], yn[:, t, :], mv[:, t, 0:1], rstd[:, t:t + 1], ALU.subtract, ALU.mult))
                link(nc.vector.tensor_tensor(yn[:, t, :], yn[:, t, :], gamma_b[0:NP, :], ALU.mult))
                link(nc.vector.tensor_tensor(yn[:, t, :], yn[:, t, :], beta_b[0:NP, :], ALU.add))
                link(nc.vector.tensor_tensor(yn[:, t, :], yn[:, t, :], x1[:, t, :], ALU.add))
            moments(3)
            for t in range(NT):
                nc.vector.tensor_scalar(yn[:, t, :], yn[:, t, :], mv[:, t, 0:1], rstd[:, t:t + 1], ALU.subtract, ALU.mult).then_inc(res_done, 1)


def kernel(**inputs):
    import numpy as np
    import concourse.bacc as bacc
    from concourse.bass_utils import run_bass_kernel_spmd

    a = {k: np.ascontiguousarray(v) for k, v in inputs.items()}
    pad = NBLK * BLK - EDGES

    def edge_tiles(v, fill):
        return np.ascontiguousarray(np.concatenate([v, np.full(pad, fill, v.dtype)]).reshape(TILES, P).T)

    def edges_last(v):
        return np.ascontiguousarray(np.concatenate([v, np.zeros((pad, v.shape[1]), v.dtype)]).T)

    l0, l1 = "L0_gnn_", "L1_gnn_"
    arrays = {
        "x": a["x"], "xT": np.ascontiguousarray(a["x"].T),
        "src": edge_tiles(a["src"], 0), "dst": edge_tiles(a["dst"], PAD_DST),
        "dst_first": np.ascontiguousarray(a["dst"][::BLK])[None, :],
        "efT": np.ascontiguousarray(edges_last(a["edge_attr_256"]).reshape(KD, P, NBLK * BLK).transpose(1, 0, 2)),
        "eaT": edges_last(a["edge_attr_64"]),
        "We1": a[l0 + "We1"], "be1": np.ascontiguousarray(a[l0 + "be1"].reshape(KH, P).T),
        "We2": a[l0 + "We2"], "be2": a[l0 + "be2"],
        "Wn1": a[l0 + "Wn1"], "bn1": np.ascontiguousarray(a[l0 + "bn1"].reshape(KH, P).T),
        "Wn2": a[l0 + "Wn2"], "bn2": a[l0 + "bn2"], "eps": a[l0 + "eps"],
        "W1": a[l1 + "W1"], "b1": a[l1 + "b1"], "W2": a[l1 + "W2"], "b2": a[l1 + "b2"][None, :],
        "Wg": a[l1 + "Wg"], "bg": a[l1 + "bg"], "gamma": a[l1 + "gamma"], "beta": a[l1 + "beta"],
    }
    nc = bacc.Bacc("TRN2", target_bir_lowering=False, num_devices=1)
    arrays = {f"in_{k}": v for k, v in arrays.items()}
    aps = [nc.dram_tensor(k, v.shape, mybir.dt.from_np(v.dtype), kind="ExternalInput").ap() for k, v in arrays.items()]
    aps.append(nc.dram_tensor("out_0", (NODES, D), F32, kind="ExternalOutput").ap())
    gnn_two_layers(nc, *aps)
    r = run_bass_kernel_spmd(nc, [arrays], core_ids=[0])
    return r.results[0]["out_0"]
```

```python
from contextlib import ExitStack

import concourse.bass as bass
from concourse import mybir

F32 = mybir.dt.float32
F32R = mybir.dt.float32r
BF16 = mybir.dt.bfloat16
I32 = mybir.dt.int32
U32 = mybir.dt.uint32
ALU = mybir.AluOpType
ACT = mybir.ActivationFunctionType
AX = mybir.AxisListType

P = 128
NODES = 625
NT = 5
NP = NODES // NT
NHALF = (320, 305)
FIN_GROUPS = ((0, 3), (3, 5))
OUT_ORDER = ((0, 0), (1, 3), (1, 4), (0, 1), (0, 2))
EDGES = 20625
BLK = 512
TPB = BLK // P
NBLK = -(-EDGES // BLK)
LAST_TILES = -(-(EDGES - (NBLK - 1) * BLK) // (2 * P)) * 2
TILES = (NBLK - 1) * TPB + LAST_TILES
FULL_TILES = EDGES // P
TAIL = EDGES - FULL_TILES * P
D = 256
KD = D // P
HID = 512
KH = HID // P
DE = 64
WIN = 64
NWIN = -(-NODES // WIN)
ACC = NODES + WIN - 1
LN_EPS = 1e-5
WARM_START, WARM_DRAIN, WARM_NODE, WARM_EDGE, WARM_SUMS = 15, 12, 9, 40, 4
PAD_DST = -100000
LAG = 5
PAIRS = (NBLK - LAG) // 2 - 1
assert LAG + 2 * PAIRS == NBLK - 2 and 2 * DE == P and TPB == 4


def run_steps(eng, step, last, first=0, pairs=PAIRS):
    for b in range(first, LAG):
        step(b, b // 2, b % 2)
    with eng.Fori(0, pairs) as i:
        step(2 * i + LAG, i + LAG // 2, LAG % 2)
        step(2 * i + LAG + 1, i + (LAG + 1) // 2, (LAG + 1) % 2)
    for b in range(LAG + 2 * pairs, last + 1):
        step(b, b // 2, b % 2)


def at_least(b, k):
    return b >= k if isinstance(b, int) else True


def inside(b):
    return 0 <= b < NBLK if isinstance(b, int) else True


def tiles_of(b):
    return LAST_TILES if isinstance(b, int) and b == NBLK - 1 else TPB


def pairs_of(b):
    return tiles_of(b) // 2


def gnn_two_layers(nc, x, xT, src, dst, dst_first, efT, eaT, We1, be1, We2, be2, Wn1, bn1, Wn2, bn2, eps,
                   W1, b1, W2, b2, Wg, bg, gamma, beta, out):
    with ExitStack() as ctx:
        def sb(name, shape, dt=F32):
            return ctx.enter_context(nc.sbuf_tensor(name, shape, dt))

        def sem(name):
            return ctx.enter_context(nc.semaphore(name))

        def two(name):
            return [sem(name + "0"), sem(name + "1")]

        xtab = nc.dram_tensor("xtab", [NODES, D], F32, kind="Internal").ap()
        ptab = nc.dram_tensor("ptab", [NODES, 2 * D], F32, kind="Internal").ap()

        we1_raw = sb("we1_raw", [P, KD, HID])
        we2_raw = sb("we2_raw", [P, KH, D])
        w2_raw = sb("w2_raw", [P, KD, D])
        wp_raw = sb("wp_raw", [P, 2 * D])
        we1 = [sb(f"we1_{n}", [P, KD, HID], F32R) for n in "hl"]
        we2 = [sb(f"we2_{n}", [P, KH, D], F32R) for n in "hl"]
        w2 = [sb(f"w2_{n}", [P, KD, D], F32R) for n in "hl"]
        wp_hi = sb("wp_hi", [P, 2 * D], F32R)
        wp = sb("wp", [P, 2 * D], F32R)
        wx = sb("wx", [P, KD, 2 * D])
        wn1 = sb("wn1", [P, KD, HID])
        wn2 = sb("wn2", [P, KH, D])
        b2pad_raw = sb("b2pad_raw", [P, D])
        b2hi = sb("b2hi", [P, D], F32R)
        b2r = sb("b2r", [P, D], F32R)
        ones_r = sb("ones_r", [P, P], F32R)
        be1c = sb("be1c", [P, KH])
        bn1c = sb("bn1c", [P, KH])
        be2b = sb("be2b", [P, D])
        bn2b = sb("bn2b", [NP, D])
        bpb = sb("bpb", [NP, 2 * D])
        ones1 = sb("ones1", [1, P])
        ones_f = sb("ones_f", [P, P])
        gamma_b = sb("gamma_b", [P, D])
        beta_b = sb("beta_b", [P, D])
        epsp1 = sb("epsp1", [P, 1])
        ident = sb("ident", [P, P])

        xn = sb("xn", [NP, NT, D])
        acc = sb("acc", [P, KD, ACC])
        hT = sb("hT", [P, KD, NODES])
        yn = sb("yn", [NP, NT, D])
        xb2 = yn
        x1 = sb("x1", [NP, NT, D])
        stats = sb("stats", [NP, NT, 6])
        mv = sb("mv", [NP, NT, 2])
        sd = sb("sd", [NP, NT])
        rstd = sb("rstd", [NP, NT])
        shift = sb("shift", [NP, NT])
        ln_eps = sb("ln_eps", [NP, 1])
        table_in = sb("table_in", [1, 1])

        src_all = sb("src_all", [P, TILES], I32)
        src_slot = sb("src_slot", [P, 2, TPB], I32)
        turn = sb("turn", [1, 1])
        dst_i = sb("dst_i", [P, TILES], I32)
        dst_f = sb("dst_f", [P, TILES])
        dst_r = sb("dst_r", [P, TILES])
        first_i = sb("first_i", [1, NBLK], I32)
        first_f = sb("first_f", [1, NBLK])
        clamp = sb("clamp", [P, TILES])
        off = sb("off", [P, 1])
        off_i = sb("off_i", [1, 1], I32)
        iota = sb("iota", [P, NWIN * WIN])

        raw = sb("raw", [P, 2, KD, BLK])
        xh = sb("xh", [P, 2, KD, BLK], F32R)
        xl = sb("xl", [P, 2, KD, BLK], F32R)
        hh = sb("hh", [P, 2, KH, BLK], F32R)
        hl = sb("hl", [P, 2, KH, BLK], F32R)
        hf = sb("hf", [P, 2, BLK])
        xg = sb("xg", [P, 2, TPB, 2 * D])
        mf_gate = sb("mf_gate", [P, 2, 2, TPB, D])
        mf = mf_gate[:, 0, :, :, :]
        gate = mf_gate[:, 1, :, :, :]
        mp = [sb(f"mp_{n}", [P, 2, TPB, D], BF16) for n in range(3)]
        r1T = xg[:, :, :, :].rearrange("p a t d -> p (a t d)")[:, 0:KH * NODES].rearrange("p (k n) -> p k n", k=KH)
        pt = mf_gate[0:NP, :, :, :, :].rearrange("p g a t d -> p (g a t d)")[:, 0:NT * 2 * D].rearrange("p (t d) -> p t d", t=NT)
        onehot = sb("onehot", [P, 2, TPB, WIN], BF16)

        bank = [ctx.enter_context(nc.psum_tensor(f"bank{i}", [P, 512], F32)) for i in range(8)]

        s_we1, s_we2, s_w2, s_wp = two("s_we1_"), sem("s_we2"), sem("s_w2"), sem("s_wp")
        s_b2, s_small, s_x, s_idx, s_src, s_nodew = sem("s_b2"), sem("s_small"), sem("s_x"), sem("s_idx"), sem("s_src"), sem("s_nodew")
        s_xtab, s_ptab, s_out = sem("s_xtab"), sem("s_ptab"), sem("s_out")
        pool_const, dve_const = sem("pool_const"), sem("dve_const")
        hi_w, lo_w = sem("hi_w"), sem("lo_w")
        xb2_ready, prep, base_ps, off_ps, flag_ready = sem("xb2_ready"), sem("prep"), sem("base_ps"), sem("off_ps"), sem("flag_ready")
        L = [{n: sem(f"{n}_l{k}") for n in
              ("hi_done", "lo_done", "h_mm", "h_evac", "hl_done", "z_mm", "window_mm", "m_done", "mp0_done", "rest_done", "mp1_done", "mp2_done",
               "slot_done", "oh_done", "acc_done", "u_mm", "rh_done", "rl_done",
               "gate_in", "gate_done", "mp2_pool", "summed", "all_summed")} for k in range(2)]
        loaded = [two("loaded_l0_"), two("loaded_l1_")]
        gathered = [two("gathered_l0_"), two("gathered_l1_")]
        acc_zero, h0_ready, n1_mm, r1_done, n2_mm, y_done, ln, sq, x1_done = (sem(n) for n in (
            "acc_zero", "h0_ready", "n1_mm", "r1_done", "n2_mm", "y_done", "ln", "sq", "x1_done"))
        lnstep, xbn2_done, x1b_done, shift_done = sem("lnstep"), sem("xbn2_done"), sem("x1b_done"), sem("shift_done")
        b2z = sem("b2z")
        xt_mm, xt_done, p_mm, p_done, fin_mm = (sem(n) for n in (
            "xt_mm", "xt_done", "p_mm", "p_done", "fin_mm"))
        res_done = two("res_done")

        block = ctx.enter_context(nc.Block())

        def all_gathered(b, half):
            return 64 * half + 16 * tiles_of(b)

        node_starts = (0, NHALF[0])
        we1_halves = (slice(0, HID // 2), slice(HID // 2, HID))

        def rows(w, n):
            return w.rearrange("(k p) n -> p k n", p=P)

        @block.sync
        def _(sp):
            def load0(b, half, q):
                if at_least(b, 2):
                    sp.wait_ge(L[0]["lo_done"], b - 1)
                sp.dma_start(raw[:, q, :, 0:tiles_of(b) * P], efT[:, :, bass.ds(b * BLK, tiles_of(b) * P)]).then_inc(loaded[0][q], 16)

            def load1(b, half, q):
                if at_least(b, 2):
                    sp.wait_ge(L[1]["lo_done"], b - 1)
                else:
                    sp.wait_ge(L[0]["lo_done"], NBLK)
                sp.dma_start(raw[0:DE, q, 0, 0:tiles_of(b) * P], eaT[:, bass.ds(b * BLK, tiles_of(b) * P)]).then_inc(loaded[1][q], 16)
                sp.dma_start(raw[DE:P, q, 0, 0:tiles_of(b) * P], eaT[:, bass.ds(b * BLK, tiles_of(b) * P)]).then_inc(loaded[1][q], 16)

            load0(0, 0, 0)
            for j, cols in enumerate(we1_halves):
                sp.dma_start(we1_raw[:, :, cols], rows(We1, HID)[:, :, cols]).then_inc(s_we1[j], 16)
            load0(1, 0, 1)
            sp.dma_start(we2_raw[:, :, :], rows(We2, D)).then_inc(s_we2, 16)
            sp.dma_start(xn[:, :, :], x.rearrange("(t p) d -> p t d", p=NP)).then_inc(s_x, 16)
            sp.dma_start(be2b[:, :], be2.partition_broadcast(P)).then_inc(s_x, 16)
            sp.wait_ge(xb2_ready, NT)
            sp.dma_start(xtab.rearrange("(t p) d -> p t d", p=NP), xb2[:, :, :]).then_inc(s_xtab, 16)
            load0(2, 1, 0)
            load0(3, 1, 1)
            sp.dma_start(w2_raw[:, :, :], rows(W2, D)).then_inc(s_w2, 16)
            for h in range(2):
                for g, w in enumerate((W1, Wg)):
                    sp.dma_start(wp_raw[h * DE:(h + 1) * DE, g * D:(g + 1) * D], w[D:D + DE, :]).then_inc(s_wp, 16)
            sp.wait_ge(pool_const, 2)
            for row in (0, 32):
                sp.dma_start(b2pad_raw[row:row + 1, :], b2).then_inc(s_b2, 16)
            for g, w in enumerate((W1, Wg)):
                sp.dma_start(wx[:, :, g * D:(g + 1) * D], rows(w[0:D, :], D)).then_inc(s_nodew, 16)
            sp.dma_start(wn1[:, :, :], rows(Wn1, HID)).then_inc(s_nodew, 16)
            sp.dma_start(wn2[:, :, :], rows(Wn2, D)).then_inc(s_nodew, 16)
            sp.dma_start(hT[:, :, :], rows(xT, NODES)).then_inc(s_nodew, 16)
            sp.dma_start(bn2b[:, :], bn2.partition_broadcast(NP)).then_inc(s_nodew, 16)
            sp.dma_start(bpb[:, 0:D], b1.partition_broadcast(NP)).then_inc(s_nodew, 16)
            sp.dma_start(bpb[:, D:2 * D], bg.partition_broadcast(NP)).then_inc(s_nodew, 16)
            sp.dma_start(gamma_b[:, :], gamma.partition_broadcast(P)).then_inc(s_nodew, 16)
            sp.dma_start(beta_b[:, :], beta.partition_broadcast(P)).then_inc(s_nodew, 16)

            run_steps(sp, load0, NBLK - 1, first=4)

            load1(0, 0, 0)
            load1(1, 0, 1)
            for t in range(NT):
                sp.wait_ge(p_done, t + 1)
                sp.dma_start(ptab[t * NP:(t + 1) * NP, :], pt[:, t, :]).then_inc(s_ptab, 16)
            run_steps(sp, load1, NBLK - 1, first=2)

            for g, t in OUT_ORDER:
                sp.wait_ge(res_done[g], t - FIN_GROUPS[g][0] + 1)
                sp.dma_start(out[t * NP:(t + 1) * NP, :], yn[:, t, :]).then_inc(s_out, 16)
            sp.wait_ge(s_out, 16 * NT)

        @block.gpsimd
        def _(pool):
            pool.dma_start(first_i[:, :], dst_first).then_inc(s_idx, 16)
            pool.dma_start(dst_i[:, :], dst).then_inc(s_idx, 16)
            pool.dma_start(src_all[:, :], src).then_inc(s_src, 16)
            def slots(k, b, q):
                nc.gpsimd.tensor_copy(src_slot[:, q, 0:tiles_of(b)], src_all[:, bass.ds(b * TPB, tiles_of(b))]).then_inc(L[k]["slot_done"], 1)

            def gather(k, b, half, q, table, width):
                if at_least(b, 2):
                    pool.wait_ge(L[k]["m_done" if k == 0 else "gate_in"], 2 * (b - 1))
                    if k == 1:
                        pool.wait_ge(L[1]["h_mm"], KD * (b - 1))
                pool.wait_ge(L[k]["slot_done"], b + 1)
                nc.gpsimd.tensor_tensor(turn[:, :], iota[0:1, 0:1], iota[0:1, 0:1], ALU.subtract)
                for t in range(tiles_of(b)):
                    nc.gpsimd.indirect_dma_start(
                        xg[:, q, t, 0:width], None, table,
                        bass.IndirectOffsetOnAxis(ap=src_slot[:, q, t:t + 1].bitcast(U32), axis=0),
                    ).then_inc(gathered[k][q], 16)
                if at_least(b, 1):
                    pool.wait_ge(gathered[k][1 - q], 64 * (half + (q == 1)))
                if not isinstance(b, int) or b + 1 < NBLK:
                    slots(k, b + 1, 1 - q)
                else:
                    slots(k, 0, 1 - q)

            def lo(k, b, q, n):
                pool.wait_ge(L[k]["hi_done"], b + 1)
                e = tiles_of(b) * P
                nc.gpsimd.tensor_tensor(xl[:, q, 0:n, 0:e], raw[:, q, 0:n, 0:e], xh[:, q, 0:n, 0:e].bitcast(F32),
                                        ALU.subtract).then_inc(L[k]["lo_done"], 1)

            def step0(b, half, q):
                gather(0, b, half, q, xtab, D)
                if not isinstance(b, int) or b + 2 < NBLK:
                    lo(0, b + 2, q, KD)

            pool.wait_ge(L[0]["lo_done"], 1)
            lo(0, 1, 1, KD)
            nc.gpsimd.iota(iota[:, :], [[1, NWIN * WIN]], base=0, channel_multiplier=0,
                           allow_small_or_imprecise_dtypes=True).then_inc(pool_const, 1)
            nc.gpsimd.memset(b2pad_raw[:, :], 0.0).then_inc(pool_const, 1)
            nc.gpsimd.memset(ident[:, :], 0.0).then_inc(pool_const, 1)
            pool.wait_ge(pool_const, 3)
            nc.gpsimd.affine_select(out=ident[:, :], in_=ident[:, :], compare_op=ALU.not_equal, fill=1.0, base=0,
                                    pattern=[[-1, P]], channel_multiplier=1).then_inc(pool_const, 1)
            nc.gpsimd.memset(acc[:, :, :], 0.0).then_inc(acc_zero, 1)
            pool.wait_ge(s_src, 16)
            slots(0, 0, 0)
            pool.wait_ge(s_xtab, 16)
            run_steps(pool, step0, NBLK - 1, pairs=PAIRS - 1)

            def part2_last(b, q):
                pool.wait_ge(L[1]["mp1_done"], 2 * b + pairs_of(b))
                t = tiles_of(b) - 1
                nc.gpsimd.tensor_tensor(mp[2][:, q, t, :], mf[:, q, t, :], mp[1][:, q, t, :],
                                        ALU.subtract).then_inc(L[1]["mp2_pool"], 1)

            def step1(b, half, q):
                if not isinstance(b, int) or b + 1 < NBLK:
                    gather(1, b + 1, half + (q == 1), 1 - q, ptab, 2 * D)
                if inside(b - 2):
                    part2_last(b - 2, q)
                if not isinstance(b, int) or b + 1 < NBLK:
                    lo(1, b + 1, 1 - q, 1)

            pool.wait_ge(gathered[0][0], all_gathered(NBLK - 1, (NBLK - 1) // 2))
            pool.wait_ge(L[0]["slot_done"], NBLK + 1)
            slots(1, 0, 0)
            lo(1, 0, 0, 1)
            pool.wait_ge(L[0]["m_done"], 2 * (NBLK - 1) + pairs_of(NBLK - 1))
            pool.wait_ge(x1_done, NT)
            pool.wait_ge(s_nodew, 16 * 10)
            nc.gpsimd.tensor_tensor(xn[:, :, :], x1[:, :, :], beta_b[0:NP, :].rearrange("p (o d) -> p o d", o=1).broadcast_to([NP, NT, D]),
                                    ALU.add).then_inc(x1b_done, 1)
            pool.wait_ge(s_ptab, 16 * NT)
            gather(1, 0, 0, 0, ptab, 2 * D)
            run_steps(pool, step1, NBLK + 1, pairs=PAIRS - 1)

        @block.scalar
        def _(act):

            def hi(k, b, half, q, n):
                act.wait_ge(loaded[k][q], (16 if k == 0 else 32) * (half + 1))
                if at_least(b, 2):
                    act.wait_ge(L[k]["h_mm" if k == 0 else "u_mm"], (b - 1) * (KH if k == 0 else 2))
                    act.wait_ge(L[k]["lo_done"], b - 1)
                elif k == 1:
                    act.wait_ge(L[0]["h_mm"], NBLK * KH)
                e = tiles_of(b) * P
                nc.scalar.activation(xh[:, q, 0:n, 0:e], raw[:, q, 0:n, 0:e], ACT.Copy).then_inc(L[k]["hi_done"], 1)

            hi(0, 0, 0, 0, KD)
            for j, cols in enumerate(we1_halves):
                act.wait_ge(s_we1[j], 16)
                nc.scalar.activation(we1[0][:, :, cols], we1_raw[:, :, cols], ACT.Copy).then_inc(hi_w, 1)
            act.dma_start(be1c[:, :], be1).then_inc(s_small, 16)
            act.dma_start(bn1c[:, :], bn1).then_inc(s_small, 16)
            act.dma_start(epsp1[:, :], eps.partition_broadcast(P)).then_inc(s_small, 16)
            hi(0, 1, 0, 1, KD)
            act.wait_ge(s_we2, 16)
            nc.scalar.activation(we2[0][:, :, :], we2_raw[:, :, :], ACT.Copy).then_inc(hi_w, 1)
            act.wait_ge(s_small, 48)

            def h_chunk(b, q, m):
                n = KH * b + m
                act.wait_ge(L[0]["h_mm"], n + 1)
                if at_least(b, 2):
                    act.wait_ge(L[0]["z_mm"], 2 * (b - 1))
                e = tiles_of(b) * P
                nc.scalar.activation(hh[:, q, m, 0:e], bank[m][:, 0:e], ACT.Relu, bias=be1c[:, m:m + 1])
                if m >= 2 or at_least(b, 1):
                    act.wait_ge(L[0]["hl_done"], n - 1)
                nc.scalar.activation(hf[:, m % 2, 0:e], bank[m][:, 0:e], ACT.Relu, bias=be1c[:, m:m + 1]).then_inc(L[0]["h_evac"], 1)

            def part0(k, b, q, c):
                tiles = slice(2 * c, 2 * c + 2)
                act.wait_ge(L[k]["m_done"], 2 * b + c + 1)
                if at_least(b, 2):
                    act.wait_ge(L[k]["summed"], b - 1)
                elif k == 1:
                    act.wait_ge(L[0]["summed"], NBLK)
                nc.scalar.activation(mp[0][:, q, tiles, :], mf[:, q, tiles, :],
                                     ACT.Relu if k == 0 else ACT.Copy).then_inc(L[k]["mp0_done"], 1)

            def part1(k, b, q, c):
                tiles = slice(2 * c, 2 * c + 2)
                act.wait_ge(L[k]["rest_done"], 2 * b + c + 1)
                nc.scalar.activation(mp[1][:, q, tiles, :], mf[:, q, tiles, :], ACT.Copy).then_inc(L[k]["mp1_done"], 1)

            def step0(b, half, q):
                second = inside(b - 2) and pairs_of(b - 2) == 2
                if second:
                    part0(0, b - 2, q, 1)
                if inside(b):
                    h_chunk(b, q, 0)
                if second:
                    part1(0, b - 2, q, 1)
                if inside(b):
                    for m in range(1, KH):
                        h_chunk(b, q, m)
                if inside(b - 1):
                    part0(0, b - 1, 1 - q, 0)
                if not isinstance(b, int) or b + 2 < NBLK:
                    hi(0, b + 2, half + 1, q, KD)
                if inside(b - 1):
                    part1(0, b - 1, 1 - q, 0)

            run_steps(act, step0, NBLK + 1, pairs=PAIRS - 1)

            act.wait_ge(s_w2, 16)
            nc.scalar.activation(w2[0][:, :, :], w2_raw[:, :, :], ACT.Copy).then_inc(hi_w, 1)
            act.wait_ge(s_wp, 64)
            nc.scalar.activation(wp_hi[:, :], wp_raw[:, :], ACT.Copy).then_inc(hi_w, 1)
            act.wait_ge(s_b2, 32)
            nc.scalar.activation(b2hi[:, :], b2pad_raw[:, :], ACT.Copy).then_inc(hi_w, 1)
            hi(1, 0, 0, 0, 1)

            for c in range(2):
                cols = slice(node_starts[c], node_starts[c] + NHALF[c])
                for m in range(KH):
                    act.wait_ge(n1_mm, KH * c + m + 1)
                    nc.scalar.activation(r1T[:, m, cols], bank[m][:, 0:NHALF[c]], ACT.Relu, bias=bn1c[:, m:m + 1]).then_inc(r1_done, 1)

            def root(n, tiles):
                act.wait_ge(ln, n)
                nc.scalar.activation(sd[:, tiles], mv[:, tiles, 1], ACT.Sqrt, bias=ln_eps[:, :]).then_inc(sq, 1)

            def x1_transposed(t):
                act.wait_ge(xt_mm, t + 1)
                nc.scalar.activation(acc[:, :, t * NP:(t + 1) * NP],
                                     bank[t % 2][:, 0:KD * P].rearrange("p (k n) -> p k n", k=KD)[:, :, 0:NP], ACT.Copy).then_inc(xt_done, 1)

            for t in range(NT):
                root(t + 1, slice(t, t + 1))
                if t >= 2:
                    x1_transposed(t - 2)
            x1_transposed(NT - 2)
            x1_transposed(NT - 1)
            nc.scalar.activation(table_in[:, :], ln_eps[0:1, :], ACT.Sigmoid)

            def gates(b, q):
                act.wait_ge(L[1]["gate_in"], 2 * b + pairs_of(b))
                n = tiles_of(b)
                nc.scalar.activation(gate[:, q, 0:n, :], gate[:, q, 0:n, :], ACT.Sigmoid).then_inc(L[1]["gate_done"], 1)

            def rh(b, q, k):
                act.wait_ge(L[1]["h_mm"], KD * b + k + 1)
                if at_least(b, 2):
                    act.wait_ge(L[1]["z_mm"], 2 * (b - 1))
                e = tiles_of(b) * P
                nc.scalar.activation(hh[:, q, k, 0:e], bank[k][:, 0:e], ACT.Relu).then_inc(L[1]["rh_done"], 1)

            def step1(b, half, q):
                if inside(b):
                    rh(b, q, 0)
                if inside(b - 2) and pairs_of(b - 2) == 2:
                    part1(1, b - 2, q, 1)
                if inside(b):
                    rh(b, q, 1)
                if not isinstance(b, int) or b + 1 < NBLK:
                    hi(1, b + 1, half + (q == 1), 1 - q, 1)
                if inside(b - 1):
                    gates(b - 1, 1 - q)
                if inside(b - 1):
                    part0(1, b - 1, 1 - q, 0)
                    if pairs_of(b - 1) == 2:
                        part0(1, b - 1, 1 - q, 1)
                    part1(1, b - 1, 1 - q, 0)

            run_steps(act, step1, NBLK + 1, pairs=PAIRS - 1)
            nc.scalar.activation(table_in[:, :], ln_eps[0:1, :], ACT.Sqrt)
            for n in range(2 * len(FIN_GROUPS)):
                first, end = FIN_GROUPS[n % len(FIN_GROUPS)]
                root(NT + n + 1, slice(first, end))
            act.wait_ge(shift_done, 1)
            for t in range(*FIN_GROUPS[0]):
                nc.scalar.activation(yn[:, t, :], yn[:, t, :], ACT.Identity, bias=shift[:, t:t + 1],
                                     scale=rstd[:, t:t + 1]).then_inc(res_done[0], 1)

        @block.tensor
        def _(pe):
            def scatter(k, b, q, gen):
                S = L[k]
                pe.wait_ge(S["mp2_done"], 2 * b + pairs_of(b))
                if k == 1:
                    pe.wait_ge(S["mp2_pool"], b + 1)
                for w in range(NWIN if gen else 1):
                    n = NWIN * b + w if gen else b
                    u = w % 2 if gen else q
                    pe.wait_ge(S["oh_done"], n + 1)
                    if at_least(b, 2) or w >= 2 or (gen and at_least(b, 1)):
                        pe.wait_ge(S["acc_done"], n - 1)
                    for f in range(KD):
                        for t in range(tiles_of(b)):
                            for part, m in enumerate(mp):
                                mm = nc.tensor.matmul(bank[6 + u][:, f * WIN:(f + 1) * WIN], m[:, q, t, f * P:(f + 1) * P],
                                                      onehot[:, u, t, :], start=(t == 0 and part == 0),
                                                      stop=(t == tiles_of(b) - 1 and part == len(mp) - 1))
                    mm.then_inc(S["summed" if w == (NWIN - 1 if gen else 0) else "window_mm"], 1)

            def h_mm(b, q, chunks=range(KH)):
                pe.wait_ge(L[0]["hi_done"], b + 1)
                pe.wait_ge(L[0]["lo_done"], b + 1)
                e = tiles_of(b) * P
                for m in chunks:
                    if at_least(b, 1):
                        pe.wait_ge(L[0]["h_evac"], KH * (b - 1) + m + 1)
                    passes = [(k, w, v) for k in range(KD) for w, v in ((0, xh), (0, xl), (1, xh))]
                    for n, (k, w, v) in enumerate(passes):
                        mm = nc.tensor.matmul(bank[m][:, 0:e], we1[w][:, k, m * P:(m + 1) * P], v[:, q, k, 0:e],
                                              start=(n == 0), stop=(n == len(passes) - 1))
                    mm.then_inc(L[0]["h_mm"], 1)

            def z_mm(b, q):
                if not at_least(b, 1):
                    pe.wait_ge(hi_w, 3)
                    pe.wait_ge(lo_w, 3)
                pe.wait_ge(L[0]["hl_done"], KH * (b + 1))
                for c in range(pairs_of(b)):
                    if at_least(b, 1):
                        pe.wait_ge(L[0]["m_done"], 2 * (b - 1) + c + 1)
                    for t in (2 * c, 2 * c + 1):
                        passes = [(k, w, v) for k in range(KH) for v, w in ((hh, 0), (hh, 1), (hl, 0))]
                        for n, (k, w, v) in enumerate(passes):
                            mm = nc.tensor.matmul(bank[4 + c][:, (t % 2) * D:(t % 2 + 1) * D], v[:, q, k, t * P:(t + 1) * P],
                                                  we2[w][:, k, :], start=(n == 0), stop=(n == len(passes) - 1))
                    mm.then_inc(L[0]["z_mm"], 1)

            def layer0(gen):
                def step(b, half, q):
                    if inside(b):
                        h_mm(b, q)
                    if inside(b - 1):
                        z_mm(b - 1, 1 - q)
                    if not inside(b - 1):
                        keep_warm(WARM_DRAIN, bank[0])
                    if inside(b - 2):
                        scatter(0, b - 2, q, gen)
                run_steps(pe, step, NBLK + 1, first=1)

            def keep_warm(n, spare=bank[7]):
                for _ in range(n):
                    nc.tensor.matmul(spare[:, 0:P], ones_f[:, :], ones_f[:, :], start=True, stop=True)

            pe.wait_ge(prep, 1)
            keep_warm(WARM_START)
            pe.wait_ge(hi_w, 1)
            pe.wait_ge(lo_w, 1)
            h_mm(0, 0, chunks=(0,))
            pe.wait_ge(prep, 2)
            nc.tensor.matmul(bank[6][:, 0:NBLK], ones1[0:1, :], first_f[0:1, :], start=True, stop=True).then_inc(base_ps, 1)
            h_mm(0, 0, chunks=(1,))
            pe.wait_ge(hi_w, 2)
            pe.wait_ge(lo_w, 2)
            h_mm(0, 0, chunks=(2,))
            pe.wait_ge(prep, 8)
            nc.tensor.matmul(bank[7][:, 0:1], ones_f[:, :], off[:, :], start=True, stop=True).then_inc(off_ps, 1)
            h_mm(0, 0, chunks=(3,))
            pe.wait_ge(flag_ready, 1)
            outside = pe.value_load(off_i[0:1, 0:1], min_val=0, max_val=1)

            with pe.If(outside < 1):
                layer0(False)
            with pe.Else():
                layer0(True)

            keep_warm(WARM_NODE, bank[0])
            pe.wait_ge(s_nodew, 16 * 10)
            for c in range(2):
                cols = slice(node_starts[c], node_starts[c] + NHALF[c])
                pe.wait_ge(h0_ready, c + 1)
                for m in range(KH):
                    if c == 1:
                        pe.wait_ge(r1_done, m + 1)
                    for k in range(KD):
                        mm = nc.tensor.matmul(bank[m][:, 0:NHALF[c]], wn1[:, k, m * P:(m + 1) * P], hT[:, k, cols],
                                              start=(k == 0), stop=(k == KD - 1))
                    mm.then_inc(n1_mm, 1)

            def n2(t):
                pe.wait_ge(r1_done, KH if (t + 1) * NP <= NHALF[0] else 2 * KH)
                if t >= 2:
                    pe.wait_ge(y_done, t - 1)
                for k in range(KH):
                    mm = nc.tensor.matmul(bank[4 + t % 2][0:NP, 0:D], r1T[:, k, t * NP:(t + 1) * NP], wn2[:, k, :],
                                          start=(k == 0), stop=(k == KH - 1))
                mm.then_inc(n2_mm, 1)

            def x1_t(t):
                pe.wait_ge(x1_done, t + 1)
                if t >= 2:
                    pe.wait_ge(xt_done, t - 1)
                for k in range(KD):
                    mm = nc.tensor.transpose(bank[t % 2][:, k * P:k * P + NP], x1[:, t, k * P:(k + 1) * P], ident[0:NP, 0:NP])
                mm.then_inc(xt_mm, 1)

            def node_products(t):
                pe.wait_ge(xt_done, t + 1)
                if t >= 2:
                    pe.wait_ge(p_done, t - 1)
                for k in range(KD):
                    mm = nc.tensor.matmul(bank[2 + t % 2][0:NP, :], acc[:, k, t * NP:(t + 1) * NP], wx[:, k, :],
                                          start=(k == 0), stop=(k == KD - 1))
                mm.then_inc(p_mm, 1)

            n2(0)
            n2(1)
            n2(2)
            x1_t(0)
            n2(3)
            x1_t(1)
            node_products(0)
            n2(4)
            x1_t(2)
            node_products(1)
            x1_t(3)
            node_products(2)
            x1_t(4)
            node_products(3)
            node_products(4)

            def th_mm(b, half, q):
                pe.wait_ge(gathered[1][q], all_gathered(b, half))
                e = tiles_of(b) * P
                for k in range(KD):
                    if at_least(b, 1):
                        pe.wait_ge(L[1]["rl_done"], KD * (b - 1) + k + 1)
                    for t in range(tiles_of(b)):
                        nc.tensor.matmul(bank[k][:, t * P:(t + 1) * P], xg[:, q, t, k * P:(k + 1) * P], ident[:, :],
                                         is_transpose=True, start=(t == 0), stop=False, skip_group_check=True)
                    if k == 0:
                        pe.wait_ge(L[1]["hi_done"], b + 1)
                        pe.wait_ge(L[1]["lo_done"], b + 1)
                    for n, v in enumerate((xh, xl)):
                        mm = nc.tensor.matmul(bank[k][:, 0:e], wp[:, k * P:(k + 1) * P], v[:, q, 0, 0:e],
                                              start=False, stop=(n == 1), skip_group_check=True)
                    mm.then_inc(L[1]["h_mm"], 1)

            def u_mm(b, q):
                if not at_least(b, 1):
                    pe.wait_ge(L[1]["hi_done"], b + 1)
                    pe.wait_ge(L[1]["lo_done"], b + 1)
                    pe.wait_ge(p_done, NT)
                for c in range(pairs_of(b)):
                    if at_least(b, 1):
                        pe.wait_ge(L[1]["gate_in"], 2 * (b - 1) + c + 1)
                    for t in (2 * c, 2 * c + 1):
                        for n, v in enumerate((xh, xl)):
                            mm = nc.tensor.matmul(bank[2 + c][:, (t % 2) * D:(t % 2 + 1) * D], v[:, q, 0, t * P:(t + 1) * P],
                                                  wp[:, D:2 * D], start=(n == 0), stop=(n == 1))
                    mm.then_inc(L[1]["u_mm"], 1)

            def c_tile(b, q, t):
                c = t // 2
                if t == 0:
                    pe.wait_ge(L[1]["rl_done"], KD * (b + 1))
                if t % 2 == 0 and at_least(b, 1):
                    pe.wait_ge(L[1]["m_done"], 2 * (b - 1) + c + 1)
                passes = [(ones_r[:, :], b2r[:, :])]
                passes += [(v[:, q, k, t * P:(t + 1) * P], w2[w][:, k, :]) for k in range(KD) for v, w in ((hh, 0), (hh, 1), (hl, 0))]
                for n, (lhs, rhs) in enumerate(passes):
                    mm = nc.tensor.matmul(bank[4 + c][:, (t % 2) * D:(t % 2 + 1) * D], lhs, rhs, start=(n == 0), stop=(n == len(passes) - 1))
                if t % 2:
                    mm.then_inc(L[1]["z_mm"], 1)

            def layer1(gen):
                def step(b, half, q):
                    if not at_least(b, 1):
                        u_mm(b, q)
                        th_mm(b, half, q)
                    elif inside(b):
                        th_mm(b, half, q)
                        u_mm(b, q)
                    if inside(b - 1):
                        for t in range(tiles_of(b - 1)):
                            c_tile(b - 1, 1 - q, t)
                    if not inside(b - 1) and at_least(b, 1):
                        keep_warm(WARM_DRAIN, bank[0])
                    if inside(b - 2):
                        scatter(1, b - 2, q, gen)
                run_steps(pe, step, NBLK + 1)

            pe.wait_ge(hi_w, 6)
            pe.wait_ge(lo_w, 6)
            keep_warm(WARM_EDGE)
            with pe.If(outside < 1):
                layer1(False)
            with pe.Else():
                layer1(True)

            keep_warm(WARM_SUMS, bank[0])
            pe.wait_ge(L[1]["all_summed"], 1)
            for t in range(NT):
                for k in range(KD):
                    mm = nc.tensor.transpose(bank[t][0:NP, k * P:(k + 1) * P], acc[:, k, t * NP:(t + 1) * NP], ident[:, :])
                mm.then_inc(fin_mm, 1)

        @block.vector
        def _(dve):
            nprep = [0]

            def p_step(ins):
                nprep[0] += 1
                ins.then_inc(prep, 1)
                dve.wait_ge(prep, nprep[0])

            nc.vector.memset(ones_f[:, :], 1.0)
            nc.vector.memset(ln_eps[:, :], LN_EPS)
            p_step(nc.vector.memset(ones1[:, :], 1.0))
            dve.wait_ge(L[0]["hi_done"], 1)
            nc.vector.tensor_tensor(xl[:, 0, :, :], raw[:, 0, :, :], xh[:, 0, :, :].bitcast(F32), ALU.subtract).then_inc(L[0]["lo_done"], 1)
            for j, cols in enumerate(we1_halves):
                dve.wait_ge(hi_w, j + 1)
                nc.vector.tensor_tensor(we1[1][:, :, cols], we1_raw[:, :, cols], we1[0][:, :, cols].bitcast(F32), ALU.subtract).then_inc(lo_w, 1)
            dve.wait_ge(s_idx, 32)
            p_step(nc.vector.tensor_copy(first_f[:, :], first_i[:, :]))
            p_step(nc.vector.tensor_copy(dst_f[:, :], dst_i[:, :]))
            dve.wait_ge(base_ps, 1)
            full = (NBLK - 1) * TPB
            nc.vector.tensor_tensor(dst_r[:, 0:full].rearrange("p (b t) -> p b t", t=TPB),
                                    dst_f[:, 0:full].rearrange("p (b t) -> p b t", t=TPB),
                                    bank[6][:, 0:NBLK - 1].rearrange("p (b o) -> p b o", o=1).broadcast_to([P, NBLK - 1, TPB]), ALU.subtract)
            p_step(nc.vector.tensor_tensor(dst_r[:, full:TILES], dst_f[:, full:TILES],
                                           bank[6][:, NBLK - 1:NBLK].broadcast_to([P, LAST_TILES]), ALU.subtract))
            p_step(nc.vector.tensor_scalar(clamp[:, :], dst_r[:, :], 0.0, float(WIN - 1), ALU.max, ALU.min))
            p_step(nc.vector.tensor_tensor(clamp[:, :], clamp[:, :], dst_r[:, :], ALU.not_equal))
            p_step(nc.vector.tensor_reduce(off[:, :], clamp[:, 0:FULL_TILES], AX.X, ALU.add))
            p_step(nc.vector.tensor_tensor(off[0:TAIL, :], off[0:TAIL, :], clamp[0:TAIL, FULL_TILES:FULL_TILES + 1], ALU.add))
            dve.wait_ge(s_x, 32)
            for t in range(NT):
                nc.vector.tensor_tensor(xb2[:, t, :], xn[:, t, :], be2b[0:NP, :], ALU.add).then_inc(xb2_ready, 1)
            dve.wait_ge(off_ps, 1)
            nc.vector.tensor_scalar(off_i[:, :], bank[7][0:1, 0:1], 1.0, None, ALU.min).then_inc(flag_ready, 1)
            dve.wait_ge(hi_w, 3)
            nc.vector.tensor_tensor(we2[1][:, :, :], we2_raw[:, :, :], we2[0][:, :, :].bitcast(F32), ALU.subtract).then_inc(lo_w, 1)

            def window_multiplied(S, b, gen, w):
                if w == (NWIN - 1 if gen else 0):
                    dve.wait_ge(S["summed"], b + 1)
                else:
                    dve.wait_ge(S["window_mm"], (NWIN - 1) * b + w + 1)

            def one_hot(k, b, q, gen, w=0):
                S = L[k]
                nt = tiles_of(b)
                u = w % 2 if gen else q
                if gen and w >= 2:
                    window_multiplied(S, b, gen, w - 2)
                elif gen and at_least(b, 1):
                    window_multiplied(S, b - 1, gen, NWIN - 2 + w)
                elif at_least(b, 2) and not gen:
                    window_multiplied(S, b - 2, gen, 0)
                which = dst_f if gen else dst_r
                nc.vector.tensor_tensor(
                    onehot[:, u, 0:nt, :],
                    iota[:, w * WIN:(w + 1) * WIN].rearrange("p (o w) -> p o w", o=1).broadcast_to([P, nt, WIN]),
                    which[:, bass.ds(b * TPB, nt)].rearrange("p (t o) -> p t o", o=1).broadcast_to([P, nt, WIN]),
                    ALU.is_equal).then_inc(S["oh_done"], 1)

            def add_window(k, b, q, gen, w=0):
                S = L[k]
                n = NWIN * b + w if gen else b
                u = w % 2 if gen else q
                first = w * WIN if gen else dve.value_load(first_i[0:1, bass.ds(b, 1)], min_val=0, max_val=NODES - 1)
                window_multiplied(S, b, gen, w)
                if w >= 1 or at_least(b, 1):
                    dve.wait_ge(S["acc_done"], n)
                elif k == 0:
                    dve.wait_ge(acc_zero, 1)
                else:
                    dve.wait_ge(xt_done, NT)
                width = min(WIN, ACC - w * WIN) if gen else WIN
                where = acc[:, :, first:first + width] if gen else acc[:, :, bass.ds(first, WIN)]
                nc.vector.tensor_tensor(
                    where, where, bank[6 + u][:, 0:KD * WIN].rearrange("p (f w) -> p f w", f=KD)[:, :, 0:width],
                    ALU.add).then_inc(S["acc_done"], 1)

            def scatter_all(k, b, q):
                for w in range(NWIN):
                    one_hot(k, b, q, True, w)
                    add_window(k, b, q, True, w)

            def hl_chunk(b, q, m):
                e = tiles_of(b) * P
                dve.wait_ge(L[0]["h_evac"], KH * b + m + 1)
                if at_least(b, 2):
                    dve.wait_ge(L[0]["z_mm"], 2 * (b - 1))
                nc.vector.tensor_tensor(hl[:, q, m, 0:e], hf[:, m % 2, 0:e], hh[:, q, m, 0:e].bitcast(F32), ALU.subtract).then_inc(L[0]["hl_done"], 1)

            def m0(b, half, q, c):
                dve.wait_ge(L[0]["z_mm"], 2 * b + c + 1)
                if c == 0:
                    dve.wait_ge(gathered[0][q], all_gathered(b, half))
                nc.vector.tensor_tensor(mf[:, q, 2 * c:2 * c + 2, :], bank[4 + c][:, :].rearrange("p (t d) -> p t d", t=2),
                                        xg[:, q, 2 * c:2 * c + 2, 0:D], ALU.add).then_inc(L[0]["m_done"], 1)

            def rest(k, b, q, c):
                tiles = slice(2 * c, 2 * c + 2)
                dve.wait_ge(L[k]["mp0_done"], 2 * b + c + 1)
                m = mf[:, q, tiles, :]
                if k == 0:
                    ins = nc.vector.scalar_tensor_tensor(out=m, in0=m, scalar=0.0, in1=mp[0][:, q, tiles, :], op0=ALU.max, op1=ALU.subtract)
                else:
                    ins = nc.vector.tensor_tensor(m, m, mp[0][:, q, tiles, :], ALU.subtract)
                ins.then_inc(L[k]["rest_done"], 1)

            def part2(k, b, q, c):
                tiles = slice(2 * c, 2 * c + 2)
                dve.wait_ge(L[k]["mp1_done"], 2 * b + c + 1)
                if k == 1 and c == pairs_of(b) - 1:
                    tiles = slice(2 * c, 2 * c + 1)
                nc.vector.tensor_tensor(mp[2][:, q, tiles, :], mf[:, q, tiles, :], mp[1][:, q, tiles, :],
                                        ALU.subtract).then_inc(L[k]["mp2_done"], 1)

            def layer0(gen):
                def step(b, half, q):
                    second = inside(b - 2) and pairs_of(b - 2) == 2
                    if second:
                        rest(0, b - 2, q, 1)
                    if inside(b):
                        hl_chunk(b, q, 0)
                    if second:
                        part2(0, b - 2, q, 1)
                    if inside(b):
                        for m in range(1, KH):
                            hl_chunk(b, q, m)
                    if inside(b - 1):
                        hb = half - (q == 0)
                        if not gen:
                            one_hot(0, b - 1, 1 - q, gen)
                        m0(b - 1, hb, 1 - q, 0)
                        rest(0, b - 1, 1 - q, 0)
                        if pairs_of(b - 1) == 2:
                            m0(b - 1, hb, 1 - q, 1)
                        part2(0, b - 1, 1 - q, 0)
                    if inside(b - 2):
                        if gen:
                            scatter_all(0, b - 2, q)
                        else:
                            add_window(0, b - 2, q, gen)
                run_steps(dve, step, NBLK + 1, first=1)
                dve.wait_ge(L[0]["acc_done"], NBLK * (NWIN if gen else 1))

            for m in range(KH):
                hl_chunk(0, 0, m)
            dve.wait_ge(s_small, 48)
            nc.vector.tensor_scalar(epsp1[:, :], epsp1[:, :], 1.0, None, ALU.add).then_inc(dve_const, 1)
            dve.wait_ge(pool_const, 1)
            dve.wait_ge(flag_ready, 1)
            outside = dve.value_load(off_i[0:1, 0:1], min_val=0, max_val=1)
            with dve.If(outside < 1):
                layer0(False)
            with dve.Else():
                layer0(True)

            dve.wait_ge(s_nodew, 16 * 10)
            dve.wait_ge(dve_const, 1)
            for c in range(2):
                cols = slice(node_starts[c], node_starts[c] + NHALF[c])
                nc.vector.scalar_tensor_tensor(out=hT[:, :, cols], in0=hT[:, :, cols], scalar=epsp1[:, 0:1], in1=acc[:, :, cols],
                                               op0=ALU.mult, op1=ALU.add).then_inc(h0_ready, 1)
            for t in range(NT):
                nc.vector.tensor_tensor(xn[:, t, :], xn[:, t, :], bn2b[:, :], ALU.add).then_inc(xbn2_done, 1)
            dve.wait_ge(hi_w, 6)
            nc.vector.tensor_tensor(w2[1][:, :, :], w2_raw[:, :, :], w2[0][:, :, :].bitcast(F32), ALU.subtract).then_inc(lo_w, 1)
            nc.vector.tensor_copy(wp[0:DE, :], wp_hi[0:DE, :].bitcast(F32))
            nc.vector.tensor_tensor(wp[DE:P, :], wp_raw[DE:P, :], wp_hi[DE:P, :].bitcast(F32), ALU.subtract).then_inc(lo_w, 1)
            nc.vector.tensor_copy(ones_r[:, :], ones_f[:, :])
            nc.vector.memset(b2r[:, :].bitcast(F32), 0.0).then_inc(b2z, 1)
            dve.wait_ge(b2z, 1)
            nc.vector.tensor_copy(b2r[0:32, :], b2hi[0:32, :].bitcast(F32))
            nc.vector.tensor_tensor(b2r[32:64, :], b2pad_raw[32:64, :], b2hi[32:64, :].bitcast(F32), ALU.subtract).then_inc(lo_w, 1)

            nln = [0]

            def link(ins):
                nln[0] += 1
                ins.then_inc(lnstep, 1)
                dve.wait_ge(lnstep, nln[0])

            def layernorm1(t):
                tile = slice(t, t + 1)
                dve.wait_ge(n2_mm, t + 1)
                ins = nc.vector.tensor_tensor(yn[:, t, :], bank[4 + t % 2][0:NP, 0:D], xn[:, t, :], ALU.add)
                ins.then_inc(y_done, 1)
                dve.wait_ge(y_done, t + 1)
                link(nc.vector.bn_stats(stats[:, t, :], yn[:, t, :]))
                nc.vector.bn_aggr(mv[:, t, :], stats[:, t, :]).then_inc(ln, 1)
                dve.wait_ge(sq, t + 1)
                link(nc.vector.reciprocal(rstd[:, tile], sd[:, tile]))
                nc.vector.tensor_scalar(x1[:, t, :], yn[:, t, :], mv[:, t, 0:1], rstd[:, tile], ALU.subtract, ALU.mult).then_inc(x1_done, 1)

            def products_out(t):
                dve.wait_ge(p_mm, t + 1)
                nc.vector.tensor_tensor(pt[:, t, :], bank[2 + t % 2][0:NP, :], bpb[:, :], ALU.add).then_inc(p_done, 1)

            dve.wait_ge(xbn2_done, NT)
            for t in range(NT - 1):
                layernorm1(t)
            products_out(0)
            layernorm1(NT - 1)
            for t in range(1, NT):
                products_out(t)

            def gate_sum(b, half, q, c):
                dve.wait_ge(L[1]["u_mm"], 2 * b + c + 1)
                if c == 0:
                    dve.wait_ge(gathered[1][q], all_gathered(b, half))
                nc.vector.tensor_tensor(gate[:, q, 2 * c:2 * c + 2, :], bank[2 + c][:, :].rearrange("p (t d) -> p t d", t=2),
                                        xg[:, q, 2 * c:2 * c + 2, D:2 * D], ALU.add).then_inc(L[1]["gate_in"], 1)

            def rl(b, q, k):
                dve.wait_ge(L[1]["rh_done"], KD * b + k + 1)
                if at_least(b, 2):
                    dve.wait_ge(L[1]["z_mm"], 2 * (b - 1))
                e = tiles_of(b) * P
                nc.vector.scalar_tensor_tensor(out=hl[:, q, k, 0:e], in0=bank[k][:, 0:e], scalar=0.0, in1=hh[:, q, k, 0:e].bitcast(F32),
                                               op0=ALU.max, op1=ALU.subtract).then_inc(L[1]["rl_done"], 1)

            def m1(b, q, c):
                dve.wait_ge(L[1]["z_mm"], 2 * b + c + 1)
                dve.wait_ge(L[1]["gate_done"], b + 1)
                if at_least(b, 2):
                    dve.wait_ge(L[1]["mp2_pool"], b - 1)
                nc.vector.tensor_tensor(mf[:, q, 2 * c:2 * c + 2, :], bank[4 + c][:, :].rearrange("p (t d) -> p t d", t=2),
                                        gate[:, q, 2 * c:2 * c + 2, :], ALU.mult).then_inc(L[1]["m_done"], 1)

            def layer1(gen):
                def step(b, half, q):
                    if inside(b):
                        rl(b, q, 0)
                    if inside(b - 2) and pairs_of(b - 2) == 2:
                        part2(1, b - 2, q, 1)
                    if inside(b):
                        rl(b, q, 1)
                        gate_sum(b, half, q, 0)
                        if pairs_of(b) == 2:
                            gate_sum(b, half, q, 1)
                    if inside(b - 1):
                        m1(b - 1, 1 - q, 0)
                        if pairs_of(b - 1) == 2:
                            m1(b - 1, 1 - q, 1)
                        if not gen:
                            one_hot(1, b - 1, 1 - q, gen)
                        rest(1, b - 1, 1 - q, 0)
                    if inside(b - 3) and not gen:
                        add_window(1, b - 3, 1 - q, gen)
                    if inside(b - 1):
                        if pairs_of(b - 1) == 2:
                            rest(1, b - 1, 1 - q, 1)
                        part2(1, b - 1, 1 - q, 0)
                    if inside(b - 2) and gen:
                        scatter_all(1, b - 2, q)
                run_steps(dve, step, NBLK + 2)

            with dve.If(outside < 1):
                layer1(False)
            with dve.Else():
                layer1(True)
            nc.vector.memset(clamp[:, :], 0.0).then_inc(L[1]["all_summed"], 1)

            def moments(tiles, value, products=False):
                for t in tiles:
                    if products:
                        dve.wait_ge(fin_mm, t + 1)
                    ins = nc.vector.bn_stats(stats[:, t, :], value(t))
                link(ins)
                for t in tiles:
                    ins = nc.vector.bn_aggr(mv[:, t, :], stats[:, t, :])
                ins.then_inc(ln, 1)

            groups = [range(first, end) for first, end in FIN_GROUPS]
            for tiles in groups:
                moments(tiles, lambda t: bank[t][0:NP, 0:D], products=True)
            dve.wait_ge(x1b_done, 1)
            for g, tiles in enumerate(groups):
                dve.wait_ge(sq, NT + g + 1)
                nc.vector.reciprocal(rstd[:, tiles[0]:tiles[-1] + 1], sd[:, tiles[0]:tiles[-1] + 1])
                for t in tiles:
                    ins = nc.vector.scalar_tensor_tensor(out=yn[:, t, :], in0=bank[t][0:NP, 0:D], scalar=mv[:, t, 0:1],
                                                         in1=gamma_b[0:NP, :], op0=ALU.subtract, op1=ALU.mult)
                link(ins)
                for t in tiles:
                    ins = nc.vector.scalar_tensor_tensor(out=yn[:, t, :], in0=yn[:, t, :], scalar=rstd[:, t:t + 1],
                                                         in1=xn[:, t, :], op0=ALU.mult, op1=ALU.add)
                link(ins)
            for tiles in groups:
                moments(tiles, lambda t: yn[:, t, :])
            for g, tiles in enumerate(groups):
                cols = slice(tiles[0], tiles[-1] + 1)
                dve.wait_ge(sq, NT + len(groups) + g + 1)
                link(nc.vector.reciprocal(rstd[:, cols], sd[:, cols]))
                if g == 0:
                    nc.vector.scalar_tensor_tensor(out=shift[:, cols], in0=mv[:, cols, 0], scalar=-1.0, in1=rstd[:, cols],
                                                   op0=ALU.mult, op1=ALU.mult).then_inc(shift_done, 1)
                    continue
                for t in tiles:
                    nc.vector.tensor_scalar(yn[:, t, :], yn[:, t, :], mv[:, t, 0:1], rstd[:, t:t + 1],
                                            ALU.subtract, ALU.mult).then_inc(res_done[1], 1)


def kernel(**inputs):
    import numpy as np
    import concourse.bacc as bacc
    from concourse.bass_utils import run_bass_kernel_spmd

    a = {k: np.ascontiguousarray(v) for k, v in inputs.items()}
    pad = TILES * P - EDGES

    def edge_tiles(v, fill):
        return np.ascontiguousarray(np.concatenate([v, np.full(pad, fill, v.dtype)]).reshape(TILES, P).T)

    def edges_last(v):
        return np.ascontiguousarray(np.concatenate([v, np.zeros((pad, v.shape[1]), v.dtype)]).T)

    l0, l1 = "L0_gnn_", "L1_gnn_"
    arrays = {
        "x": a["x"], "xT": np.ascontiguousarray(a["x"].T),
        "src": edge_tiles(a["src"], 0), "dst": edge_tiles(a["dst"], PAD_DST),
        "dst_first": np.ascontiguousarray(a["dst"][::BLK])[None, :],
        "efT": np.ascontiguousarray(edges_last(a["edge_attr_256"]).reshape(KD, P, TILES * P).transpose(1, 0, 2)),
        "eaT": edges_last(a["edge_attr_64"]),
        "We1": a[l0 + "We1"], "be1": np.ascontiguousarray(a[l0 + "be1"].reshape(KH, P).T),
        "We2": a[l0 + "We2"], "be2": a[l0 + "be2"],
        "Wn1": a[l0 + "Wn1"], "bn1": np.ascontiguousarray(a[l0 + "bn1"].reshape(KH, P).T),
        "Wn2": a[l0 + "Wn2"], "bn2": a[l0 + "bn2"], "eps": a[l0 + "eps"],
        "W1": a[l1 + "W1"], "b1": a[l1 + "b1"], "W2": a[l1 + "W2"], "b2": a[l1 + "b2"][None, :],
        "Wg": a[l1 + "Wg"], "bg": a[l1 + "bg"], "gamma": a[l1 + "gamma"], "beta": a[l1 + "beta"],
    }
    nc = bacc.Bacc("TRN2", target_bir_lowering=False, num_devices=1)
    arrays = {f"in_{k}": v for k, v in arrays.items()}
    aps = [nc.dram_tensor(k, v.shape, mybir.dt.from_np(v.dtype), kind="ExternalInput").ap() for k, v in arrays.items()]
    aps.append(nc.dram_tensor("out_0", (NODES, D), F32, kind="ExternalOutput").ap())
    gnn_two_layers(nc, *aps)
    r = run_bass_kernel_spmd(nc, [arrays], core_ids=[0])
    return r.results[0]["out_0"]
```
